# Optimizing a Trainium2 kernel written in Bass

```python
import numpy as np
import jax
import jax.numpy as jnp

def _softmax(x, axis=-1):
    return jax.nn.softmax(x, axis=axis)

def _gelu(x):
    return jax.nn.gelu(x, approximate=True)

def _silu(x):
    return jax.nn.silu(x)

def _sigmoid(x):
    return jax.nn.sigmoid(x)

def _layernorm(x, axis=-1, eps=1e-05):
    m = jnp.mean(x, axis=axis, keepdims=True)
    v = jnp.var(x, axis=axis, keepdims=True)
    return (x - m) / jnp.sqrt(v + eps)

def _scatter_add(tgt, idx, src, axis=0):
    return tgt.at[idx].add(src)

def _segment_sum(src, seg, n):
    return jax.ops.segment_sum(src, seg, n)
kernel_name = 'mk_gnn_ffn_d1_gnn_r16_3cc95a'

def setup_inputs(seed: int=0):
    np.random.seed(seed)
    _w = jnp.asarray

    def _rec_inputs():
        import jax
        import jax.numpy as jnp
        _gk = jax.random.key(seed)
        x = -0.0001126 + 1 * jax.random.normal(jax.random.fold_in(_gk, 1), (625, 768), jnp.float32)
        src = jax.random.randint(jax.random.fold_in(_gk, 2), (10000,), 0, 625, jnp.int32)
        dst = jax.random.randint(jax.random.fold_in(_gk, 3), (10000,), 0, 625, jnp.int32)
        _o = jnp.argsort(dst, stable=True)
        src = src[_o]
        dst = dst[_o]
        return (x, src, dst)
    x, src, dst = _rec_inputs()

    def _L0_gnn_setup():
        import jax, jax.numpy as jnp
        import numpy as np
        N_NODES = 625
        D = 768
        N_EDGES = 10000

        def gcn_conv(x, W, b, src, dst, n_nodes):
            h = x @ W
            deg = jax.ops.segment_sum(jnp.ones_like(dst, dtype=h.dtype), dst, num_segments=n_nodes)
            dinv = jnp.where(deg > 0, jax.lax.rsqrt(deg), 0.0)
            norm = dinv[src] * dinv[dst]
            msgs = h[src] * norm[:, None]
            out = jax.ops.segment_sum(msgs, dst, num_segments=n_nodes)
            return out + b

        def add_self_loops(edge_index, n_nodes):
            loop = jnp.arange(n_nodes, dtype=edge_index.dtype)
            src = jnp.concatenate([edge_index[0], loop])
            dst = jnp.concatenate([edge_index[1], loop])
            return (src, dst)
        key = jax.random.key(seed)
        k1, k2, k3, k4 = jax.random.split(key, 4)
        x = jax.random.normal(k1, (N_NODES, D), dtype=jnp.float32)
        edge_index = jax.random.randint(k2, (2, N_EDGES), 0, N_NODES, dtype=jnp.int32)
        glorot = float(np.sqrt(6.0 / (D + D)))
        W1 = jax.random.uniform(k3, (D, D), jnp.float32, -glorot, glorot)
        W2 = jax.random.uniform(k4, (D, D), jnp.float32, -glorot, glorot)
        b1 = jnp.zeros((D,), jnp.float32)
        b2 = jnp.zeros((D,), jnp.float32)
        return {'x': x, 'W1': W1, 'b1': b1, 'W2': W2, 'b2': b2, 'edge_index': edge_index}
    _L0_gnn_all = _L0_gnn_setup()
    _L0_gnn_in = {k: v for k, v in _L0_gnn_all.items() if k in ('W1', 'b1', 'W2', 'b2')}
    del _L0_gnn_all

    def _L0_ffn_setup():
        import jax, jax.numpy as jnp
        import numpy as np
        B, T, D = (2, 1024, 768)
        H, HS = (12, 64)
        E, K = (8, 1)
        DF = 4 * D
        EPS = 1e-05

        def _ln(x, g, b):
            mu = jnp.mean(x, axis=-1, keepdims=True)
            var = jnp.mean(jnp.square(x - mu), axis=-1, keepdims=True)
            return (x - mu) * jax.lax.rsqrt(var + EPS) * g + b
        key = jax.random.key(seed)
        ks = jax.random.split(key, 12)
        s = 0.02
        return {'x': jax.random.normal(ks[0], (B, T, D), dtype=jnp.float32), 'ln1_g': jnp.ones((D,), jnp.float32), 'ln1_b': jnp.zeros((D,), jnp.float32), 'ln2_g': jnp.ones((D,), jnp.float32), 'ln2_b': jnp.zeros((D,), jnp.float32), 'Wq': jax.random.normal(ks[1], (H, D, HS), jnp.float32) * s, 'Wk': jax.random.normal(ks[2], (H, D, HS), jnp.float32) * s, 'Wv': jax.random.normal(ks[3], (H, D, HS), jnp.float32) * s, 'Wp': jax.random.normal(ks[4], (D, D), jnp.float32) * s, 'bp': jnp.zeros((D,), jnp.float32), 'Wg': jax.random.normal(ks[5], (D, E), jnp.float32) * s, 'W1': jax.random.normal(ks[6], (E, D, DF), jnp.float32) * s, 'b1': jnp.zeros((E, DF), jnp.float32), 'W2': jax.random.normal(ks[7], (E, DF, D), jnp.float32) * s, 'b2': jnp.zeros((E, D), jnp.float32)}
    _L0_ffn_all = _L0_ffn_setup()
    _L0_ffn_in = {k: v for k, v in _L0_ffn_all.items() if k in ('ln1_g', 'ln1_b', 'ln2_g', 'ln2_b', 'Wq', 'Wk', 'Wv', 'Wp', 'bp', 'Wg', 'W1', 'b1', 'W2', 'b2')}
    del _L0_ffn_all
    return {'x': x, 'src': src, 'dst': dst, 'L0_gnn_W1': _L0_gnn_in['W1'], 'L0_gnn_b1': _L0_gnn_in['b1'], 'L0_gnn_W2': _L0_gnn_in['W2'], 'L0_gnn_b2': _L0_gnn_in['b2'], 'L0_ffn_ln1_g': _L0_ffn_in['ln1_g'], 'L0_ffn_ln1_b': _L0_ffn_in['ln1_b'], 'L0_ffn_ln2_g': _L0_ffn_in['ln2_g'], 'L0_ffn_ln2_b': _L0_ffn_in['ln2_b'], 'L0_ffn_Wq': _L0_ffn_in['Wq'], 'L0_ffn_Wk': _L0_ffn_in['Wk'], 'L0_ffn_Wv': _L0_ffn_in['Wv'], 'L0_ffn_Wp': _L0_ffn_in['Wp'], 'L0_ffn_bp': _L0_ffn_in['bp'], 'L0_ffn_Wg': _L0_ffn_in['Wg'], 'L0_ffn_W1': _L0_ffn_in['W1'], 'L0_ffn_b1': _L0_ffn_in['b1'], 'L0_ffn_W2': _L0_ffn_in['W2'], 'L0_ffn_b2': _L0_ffn_in['b2']}

def reference(x, src, dst, L0_gnn_W1, L0_gnn_b1, L0_gnn_W2, L0_gnn_b2, L0_ffn_ln1_g, L0_ffn_ln1_b, L0_ffn_ln2_g, L0_ffn_ln2_b, L0_ffn_Wq, L0_ffn_Wk, L0_ffn_Wv, L0_ffn_Wp, L0_ffn_bp, L0_ffn_Wg, L0_ffn_W1, L0_ffn_b1, L0_ffn_W2, L0_ffn_b2):
    import jax
    import jax.numpy as jnp

    def _L0_gnn_ref(x, W1, b1, W2, b2, edge_index):
        import jax, jax.numpy as jnp
        import numpy as np
        N_NODES = 625
        D = 768
        N_EDGES = 10000

        def gcn_conv(x, W, b, src, dst, n_nodes):
            h = x @ W
            deg = jax.ops.segment_sum(jnp.ones_like(dst, dtype=h.dtype), dst, num_segments=n_nodes)
            dinv = jnp.where(deg > 0, jax.lax.rsqrt(deg), 0.0)
            norm = dinv[src] * dinv[dst]
            msgs = h[src] * norm[:, None]
            out = jax.ops.segment_sum(msgs, dst, num_segments=n_nodes)
            return out + b

        def add_self_loops(edge_index, n_nodes):
            loop = jnp.arange(n_nodes, dtype=edge_index.dtype)
            src = jnp.concatenate([edge_index[0], loop])
            dst = jnp.concatenate([edge_index[1], loop])
            return (src, dst)
        n = x.shape[0]
        src, dst = add_self_loops(edge_index, n)
        h = gcn_conv(x, W1, b1, src, dst, n)
        h = jax.nn.relu(h)
        out = gcn_conv(h, W2, b2, src, dst, n)
        return out

    def _L0_ffn_ref(x, ln1_g, ln1_b, ln2_g, ln2_b, Wq, Wk, Wv, Wp, bp, Wg, W1, b1, W2, b2):
        import jax, jax.numpy as jnp
        import numpy as np
        B, T, D = (2, 1024, 768)
        H, HS = (12, 64)
        E, K = (8, 1)
        DF = 4 * D
        EPS = 1e-05

        def _ln(x, g, b):
            mu = jnp.mean(x, axis=-1, keepdims=True)
            var = jnp.mean(jnp.square(x - mu), axis=-1, keepdims=True)
            return (x - mu) * jax.lax.rsqrt(var + EPS) * g + b
        b, t, d = x.shape
        h = _ln(x, ln1_g, ln1_b)
        q = jnp.einsum('btd,hds->bhts', h, Wq)
        k = jnp.einsum('btd,hds->bhts', h, Wk)
        v = jnp.einsum('btd,hds->bhts', h, Wv)
        scores = jnp.einsum('bhts,bhus->bhtu', q, k) * d ** (-0.5)
        causal = jnp.tril(jnp.ones((t, t), dtype=bool))
        scores = jnp.where(causal, scores, -jnp.inf)
        att = jax.nn.softmax(scores, axis=-1)
        out = jnp.einsum('bhtu,bhus->bhts', att, v)
        out = out.transpose(0, 2, 1, 3).reshape(b, t, d)
        x = x + out @ Wp + bp
        h2 = _ln(x, ln2_g, ln2_b).reshape(-1, d)
        gate_logits = h2 @ Wg
        w, sel = jax.lax.top_k(gate_logits, K)
        w = jax.nn.softmax(w.astype(jnp.float32), axis=-1).astype(x.dtype)
        n = h2.shape[0]
        combine = jnp.zeros((n, Wg.shape[1]), x.dtype).at[jnp.arange(n)[:, None], sel].add(w)
        hid = jax.nn.relu(jnp.einsum('nd,edf->enf', h2, W1) + b1[:, None, :])
        y = jnp.einsum('enf,efd->end', hid, W2) + b2[:, None, :]
        moe = jnp.einsum('ne,end->nd', combine, y)
        return x + moe.reshape(b, t, d)
    edge_index = jnp.stack([src, dst])
    x = x + _L0_gnn_ref(_layernorm(x, axis=-1), L0_gnn_W1, L0_gnn_b1, L0_gnn_W2, L0_gnn_b2, edge_index)
    x = x + _L0_ffn_ref(_layernorm(x, axis=-1)[None], L0_ffn_ln1_g, L0_ffn_ln1_b, L0_ffn_ln2_g, L0_ffn_ln2_b, L0_ffn_Wq, L0_ffn_Wk, L0_ffn_Wv, L0_ffn_Wp, L0_ffn_bp, L0_ffn_Wg, L0_ffn_W1, L0_ffn_b1, L0_ffn_W2, L0_ffn_b2)[0]
    return x

_drawn_inputs = setup_inputs


def setup_inputs(seed=0):
    import zlib

    import numpy as np

    out = dict(_drawn_inputs(seed))
    spreads = {'L0_gnn_b1': (0.0, 0.1),
     'L0_gnn_b2': (0.0, 0.1),
     'L0_ffn_ln1_g': (1.0, 0.2),
     'L0_ffn_ln1_b': (0.0, 0.1),
     'L0_ffn_ln2_g': (1.0, 0.2),
     'L0_ffn_ln2_b': (0.0, 0.1),
     'L0_ffn_bp': (0.0, 0.1),
     'L0_ffn_b1': (0.0, 0.1),
     'L0_ffn_b2': (0.0, 0.1)}
    factors = {'L0_ffn_Wq': 3.51, 'L0_ffn_Wk': 4.282}
    for name, (base, spread) in spreads.items():
        noise = np.random.default_rng([zlib.crc32(name.encode()), seed]).standard_normal(out[name].shape)
        drawn = base * np.exp(spread * noise) if base else spread * noise
        out[name] = jnp.asarray(drawn.astype(out[name].dtype))
    for name, factor in factors.items():
        out[name] = (out[name] * factor).astype(out[name].dtype)
    return out
```

```python
from contextlib import ExitStack

import concourse.bass as bass
from concourse import mybir

F32 = mybir.dt.float32
F32R = mybir.dt.float32r
BF16 = mybir.dt.bfloat16
F16 = mybir.dt.float16
I32 = mybir.dt.int32
U32 = mybir.dt.uint32
ALU = mybir.AluOpType
ACT = mybir.ActivationFunctionType
AX = mybir.AxisListType.X

N, D = 625, 768
NE = 10000
H, HS = 12, 64
E, DF = 8, 3072
EPS = 1e-5

P = 125
C = N // P
HALF = 314
NP = 2 * HALF
DC = D // 128
HB = D // 2
PAIRS = H // 2

BIG = 4096
DECODE_BUSY, DEG_BUSY = 40, 10
EC = NE // P
EU = 4
GROUPS = [8, 8, EC // EU - 16]
RADIX = 4096

CAP = 128
K_OVER = N // CAP
TILES = E + K_OVER

CH = 3 * D
FCH = DF // (CH // DC)
FW = CH // DC
JW = FW // 128
SCH = 2 * FCH
AHEAD = 3
SLOTS = 4
RAWS = 4
GNN1, GNN2, WQ, WK, WV, WP = range(6)
FRONT = 12
F_SLOTS, F_RAWS = 3, 2


def pairs(hi_lo_a, hi_lo_b):
    (ah, al), (bh, bl) = hi_lo_a, hi_lo_b
    return ((ah, bh), (ah, bl), (al, bh))


def build(nc, x, src, dst, gW1, gb1, gW2, gb2, ln1_g, ln1_b, ln2_g, ln2_b,
          Wq, Wk, Wv, Wp, bp, Wg, W1, b1, W2, b2, out):
    ctx = ExitStack()
    with ctx:
        def sb(name, shape, dt, stack=ctx):
            return stack.enter_context(nc.sbuf_tensor(name, shape, dt))

        def sem(name):
            return ctx.enter_context(nc.semaphore(name))

        def region(name, size, *variants):
            made = {}
            for variant in variants:
                with ExitStack() as s:
                    for n, shape, dt in variant:
                        made[n] = sb(n, shape, dt, s)
            sb(name, [128, size], F32)
            return made

        x1_d = nc.dram_tensor("x1_d", (N, D), F32, kind="Internal").ap()
        xf_d = nc.dram_tensor("xf_d", (N, D), F32, kind="Internal").ap()
        hs_d = nc.dram_tensor("hs_d", ((TILES + 1) * CAP, D), F32, kind="Internal").ap()
        ys_d = nc.dram_tensor("ys_d", ((TILES + 1) * CAP, D), F32, kind="Internal").ap()

        ident = sb("ident", [128, 128], F32)
        identb = sb("identb", [128, 128], BF16)
        cmask = sb("cmask", [P, 126], BF16)
        before = sb("before", [P, P], BF16)
        onesb = sb("onesb", [P, P], BF16)

        tri8 = sb("tri8", [P, E, E], F32)
        iota8 = sb("iota8", [P, E], F32)
        capk = sb("capk", [P, K_OVER], F32)
        lnT = sb("lnT", [128, 4 * DC], F32)
        rows = sb("rows", [4 * DC, 128], F32)
        b1T = sb("b1T", [128, E * DF // 128], F32)
        wg = sb("wg", [128, DC, E], F32)
        bc = [sb(f"bc{i}", [P, D], F32) for i in range(2)]
        onesr = sb("onesr", [P, 2], F32R)
        big = sb("big", [P, 2], BF16)
        bigi = sb("bigi", [1, 2], I32)
        stats = sb("stats", [P, C, 2, 6], F32)
        mvx = sb("mvx", [P, C, 2], F32)
        rx = sb("rx", [P, 2, C], F32)
        mv = sb("mv", [P, 2], F32)
        rstd = sb("rstd", [P, 1], F32)
        var = sb("var", [P, C], F32)
        root = sb("root", [P, C], F32)
        newt = sb("newt", [P, C], F32)
        dinv = sb("dinv", [P, C], F32)
        dtmp = sb("dtmp", [P, 2, C], F32)
        negmax = sb("negmax", [P, 2, 1], F32)
        smax = sb("smax", [P, 2, 1], F32)
        ssum = sb("ssum", [P, 2, 1], F32)
        rsum = sb("rsum", [P, 2, 1], F32)
        wtok = sb("wtok", [P, C], F32)
        eidx = sb("eidx", [P, C], I32)
        slot = sb("slot", [P, C], I32)
        slot1 = sb("slot1", [P, C], I32)
        over = sb("over", [1, 1 + K_OVER], I32)

        raw = [sb(f"raw{i}", [128, CH], F32) for i in range(F_RAWS)]
        whi = [sb(f"whi{i}", [128, CH], F32R) for i in range(F_SLOTS)]
        wlo = [sb(f"wlo{i}", [128, CH], F32R) for i in range(F_SLOTS)]

        RB = 7680
        R0 = region("r0", RB + 512,
                    [("S", [P, C, NP], I32), ("ohs", [P, EU, 626], BF16), ("ohd", [P, EU, HALF], BF16),
                     ("zero", [128, D], F32)],
                    [("agh", [128, DC, NP], F32R), ("agl", [128, DC, NP], F32R)],
                    [("hTh", [128, DC, NP], F32R), ("hTl", [128, DC, NP], F32R)],
                    [("pr", [P, 3, NP - 2], F32), ("pTh", [P, C, NP], F32R), ("pTl", [P, C, NP], F32R)],
                    [("raw2", [128, CH], F32), ("raw3", [128, CH], F32),
                     ("hid", [128, 2, FW], F32), ("bia", [128, 2, JW, CAP], F32), ("ysb", [128, D], F32),
                     ("rt", [P, 10, 48], F32), ("tp", [P, E, E], F32)])
        R1 = region("r1", RB,
                    [("xnh", [P, C, D], F32R), ("xnl", [P, C, D], F32R)],
                    [("xf", [P, C, D], F32), ("n1", [P, C, D], F32)],
                    [("qh", [128, PAIRS, NP], F32R), ("ql", [128, PAIRS, NP], F32R)],
                    [("whi3", [128, CH], F32R), ("wlo3", [128, CH], F32R),
                     ("hs", [128, D], F32), ("hgf", [128, DC, CAP], F32),
                     ("hgh", [128, DC, CAP], F32R), ("hgl", [128, DC, CAP], F32R)])
        R2 = region("r2", RB,
                    [("cint", [P, C, HALF], I32), ("clo", [P, C, HALF], I32), ("chi", [P, C, HALF], I32),
                     ("ei", [P, 2, EC], I32), ("ef", [P, 4, EC], F32), ("iota16", [P, 626], F16)],
                    [("Sh", [P, C, NP], F32R), ("Sl", [P, C, NP], F32R)],
                    [("kh", [128, PAIRS, NP], F32R), ("kl", [128, PAIRS, NP], F32R)],
                    [("x2", [P, C, D], F32), ("base", [P, C, D], F32)])
        R3 = region("r3", RB,
                    [("xs", [P, C, D], F32), ("tmp", [P, 2, D], F32), ("aff", [128, 2, DC, P], F32),
                     ("b1r", [96, 2, 128], F32)],
                    [("vh", [P, C, D], F32R), ("vl", [P, C, D], F32R)],
                    [("n2", [P, C, D], F32), ("h2T", [128, DC, NP], F32)],
                    [("hTTh", [128, DF // 128, CAP], F32R), ("hTTl", [128, DF // 128, CAP], F32R)])
        raw += [R0["raw2"], R0["raw3"]]
        whi += [R1["whi3"]]
        wlo += [R1["wlo3"]]
        S, ohs, ohd = R0["S"], R0["ohs"], R0["ohd"]
        ag = (R0["agh"], R0["agl"])
        hT = (R0["hTh"], R0["hTl"])
        pr, pT = R0["pr"], (R0["pTh"], R0["pTl"])
        hid, bia, ysb = R0["hid"], R0["bia"], R0["ysb"]
        xn = (R1["xnh"], R1["xnl"])
        xf, n1 = R1["xf"], R1["n1"]
        q = (R1["qh"], R1["ql"])
        hs, hgf, hg = R1["hs"], R1["hgf"], (R1["hgh"], R1["hgl"])
        cint, clo, chi, ei, ef = (R2[n] for n in ("cint", "clo", "chi", "ei", "ef"))
        iota16 = R2["iota16"]
        Sd = (R2["Sh"], R2["Sl"])
        k_ = (R2["kh"], R2["kl"])
        x2, base = R2["x2"], R2["base"]
        xs, tmp, aff, b1r = R3["xs"], R3["tmp"], R3["aff"], R3["b1r"]
        v = (R3["vh"], R3["vl"])
        n2, h2T = R3["n2"], R3["h2T"]
        rt, tp = R0["rt"], R0["tp"]
        hTT = (R3["hTTh"], R3["hTTl"])

        ps = ctx.enter_context(nc.psum_tensor("ps", [128, 8, 512], F32))

        def two(b, rows_=128):
            return ps[0:rows_, b:b + 2, 0:HALF]

        def wide(b, rows_):
            return ps[0:rows_, b:b + 2, 0:HB]

        def halves(t):
            return t.rearrange("p (a b) -> p a b", a=2)

        def blocks(b, rows_, n, width=128):
            flat = ps[0:rows_, b:b + 2, :].rearrange("p a b -> p (a b)")
            return flat[:, 0:n * 128].rearrange("p (n w) -> p n w", w=128)[:, :, 0:width]

        def turned_parts(u):
            c, nb = u % C, min(u % C + 1, 4)
            parts = [(blocks(4 + u % 2, P, nb, P), 0, nb)]
            if c == 4:
                parts.append((ps[0:P, 6:7, 384:384 + P], 4, 1))
            return parts

        def score_banks(u):
            h, c = divmod(u, C)
            return (c + 2 * (h % 2)) % 4

        def score_rows(u):
            b = score_banks(u)
            if u % C < 4:
                return ps[0:P, b, :]
            return ps[0:P, b:b + 2, :].rearrange("p a b -> p (a b)")

        UNITS = H * C

        s_edges, s_x, s_rows, s_b1r, s_wg, s_bc = (sem(n) for n in
                                                   ("edges_in", "x_in", "rows_in", "b1_in", "wg_in", "bias_in"))
        s_bp = sem("bp_in")
        s_zero, s_x1st, s_xfst, s_xfld, s_x1ld = (sem(n) for n in
                                                  ("hs_zeroed", "x1_stored", "xf_stored", "xf_back", "x1_back"))
        s_const, s_pool = sem("consts_made"), sem("pool_steps")
        s_raw = [sem(f"raw_in{i}") for i in range(RAWS)]
        s_fhi, s_flo0, s_flo = sem("front_hi"), sem("front_lo_first"), sem("front_lo")
        s_var, s_root = sem("variances_made"), sem("roots_made")
        s_vec, s_act = sem("vector_steps"), sem("scalar_steps")
        s_ef, s_oh, s_ohused = sem("edge_columns"), sem("onehots_made"), sem("onehots_used")
        s_cint, s_cdec, s_cadd = sem("counts_read"), sem("counts_decoded"), sem("counts_added")
        s_busy, s_big, s_bigs, s_bigi = (sem(n) for n in ("ones_made", "big_marked", "big_summed", "big_known"))
        s_S, s_deg, s_dinv, s_Shi, s_Slo = (sem(n) for n in ("adj_made", "deg_done", "dinv_made", "adj_hi", "adj_lo"))
        s_ln0, s_xnh, s_xnl, s_xb = (sem(n) for n in ("x_normed", "xn_hi", "xn_lo", "x_plus_b2"))
        s_misc, s_miscev = sem("vectors_turned"), sem("vectors_read")
        s_agg, s_aggh, s_aggl = sem("aggregated"), sem("agg_hi", ), sem("agg_lo")
        s_tb, s_xw, s_t, s_hh, s_hl = sem("hidden_biased"), sem("transformed"), sem("hidden_scaled"), sem("hidden_hi"), sem("hidden_lo")
        s_x1, s_xf, s_n1, s_xfb = sem("x1_made"), sem("xf_made"), sem("n1_made"), sem("xf_plus_bp")
        s_n1T, s_aff, s_hTh, s_hTl, s_pad = (sem(n) for n in ("n1_turned", "h_scaled", "hT_hi", "hT_lo", "hT_padded"))
        s_pj, s_pjh, s_pjl = sem("projected"), sem("projected_hi"), sem("projected_lo")
        s_sc, s_rmx, s_mx, s_ex, s_rs, s_nm = (sem(n) for n in ("scores_done", "max_made", "max_scaled", "exp_made", "sum_inverted", "probs_normed"))
        s_tr, s_trh, s_trl, s_pv, s_pvh, s_pvl = (sem(n) for n in (
            "probs_turned", "probs_hi", "probs_lo", "heads_done", "heads_hi", "heads_lo"))
        s_ptz = sem("probs_padded")
        s_wp, s_x2, s_base, s_n2, s_n2T, s_h2T, s_gate = (sem(n) for n in (
            "attn_projected", "x2_made", "base_made", "n2_made", "n2_turned", "h2T_made", "gates_done"))
        s_slot, s_oh8, s_rank, s_route = sem("rows_chosen"), sem("choice_made"), sem("ranks_done"), sem("routed")
        s_scat, s_b2g, s_base2 = sem("tokens_sent"), sem("b2_in"), sem("base_with_b2")
        s_hs, s_hgT, s_hga, s_hgh, s_hgl = (sem(n) for n in (
            "tile_in", "tile_turned", "tile_scaled", "tile_hi", "tile_lo"))
        s_used, s_mhi, s_mlo = (sem(n) for n in ("chunks_used", "expert_hi", "expert_lo"))
        s_hidev, s_hidT, s_bia, s_hTh2, s_hTl2 = (sem(n) for n in (
            "hid_read", "hid_turned", "hid_biased", "hidT_hi", "hidT_lo"))
        s_yev, s_yst, s_ylast, s_zt, s_yg, s_fin, s_out = (sem(n) for n in (
            "y_read", "y_stored", "last_y_stored", "zeros_made", "y_back", "out_made", "out_stored"))

        tok = lambda a: a.rearrange("(c p) d -> p c d", p=P)
        mat = lambda a: a.rearrange("(c p) f -> p c f", p=128)
        head = lambda a: a.rearrange("h (c p) s -> c p h s", p=128)
        W1v = W1.rearrange("e (c p) f -> e p c f", p=128)
        W2v = W2.rearrange("e (j p) d -> e p j d", p=128)
        edge = lambda a: a.rearrange("(p c) -> p c", p=P)
        row = lambda a: a.rearrange("(a n) -> a n", a=1)
        rowc = lambda a: a.rearrange("(c p) -> c p", p=128)

        def wview(t):
            return t[:, :].rearrange("p (c f) -> p c f", c=3)

        class Count:
            def __init__(self, eng, s):
                self.eng, self.s, self.n = eng, s, 0

            def __call__(self, ins):
                self.n += 1
                ins.then_inc(self.s, 1)
                self.eng.wait_ge(self.s, self.n)

        def split(n):
            return (s_flo0, n) if n <= F_SLOTS else (s_flo, n - F_SLOTS)

        USED = {GNN1: (s_xw, C), GNN2: (s_xw, 2 * C), WQ: (s_pj, PAIRS), WK: (s_pj, 2 * PAIRS),
                WV: (s_pj, 2 * PAIRS + C), WP: (s_wp, C)}

        def raw_value(n):
            total = 0
            for m in range(n % F_RAWS, n + 1, F_RAWS):
                total += 48 if m // 2 in (WQ, WK, WV) else 16
            return total

        FULL = [raw_value(FRONT - 2), raw_value(FRONT - 1), 0, 0]

        block = ctx.enter_context(nc.Block())

        @block.sync
        def _(sp):
            sp.dma_start(ei[:, 0, :], edge(src)).then_inc(s_edges, 16)
            sp.dma_start(ei[:, 1, :], edge(dst)).then_inc(s_edges, 16)
            sp.dma_start(xs[:, :, :], tok(x)).then_inc(s_x, 16)
            for i, a in enumerate((ln1_g, ln1_b, ln2_g, ln2_b)):
                sp.dma_start(rows[i * DC:(i + 1) * DC, :], rowc(a)).then_inc(s_rows, 16)
            for i in range(2):
                sp.dma_start(b1r[:, i, :], b1.rearrange("e (j p) -> (e j) p", p=128)[96 * i:96 * i + 96, :]
                             ).then_inc(s_b1r, 16)
            sp.dma_start(wg[:, :, :], mat(Wg)).then_inc(s_wg, 16)

            mats = (gW1, gW2, Wq, Wk, Wv, Wp)
            for n in range(FRONT):
                m, half = divmod(n, 2)
                r = raw[n % F_RAWS]
                if n >= F_RAWS:
                    sp.wait_ge(*split(n - F_RAWS + 1))
                if m in (WQ, WK, WV):
                    for c in range(3):
                        sp.dma_start(wview(r)[:, c, :].rearrange("p (h s) -> p h s", h=H),
                                     head(mats[m])[3 * half + c]).then_inc(s_raw[n % F_RAWS], 16)
                else:
                    sp.dma_start(wview(r), mat(mats[m])[:, 3 * half:3 * half + 3, :]
                                 ).then_inc(s_raw[n % F_RAWS], 16)

            def weights(e, t):
                for n in range(SCH):
                    if not isinstance(t, int) or n >= RAWS:
                        sp.wait_ge(s_mlo, SCH * t + n + 1 - RAWS)
                    elif n < F_RAWS:
                        sp.wait_ge(*split(FRONT - F_RAWS + n + 1))
                    else:
                        sp.wait_ge(s_pv, 2 * H)
                    r = raw[n % RAWS]
                    if n < FCH:
                        sp.dma_start(r[:, :].rearrange("p (c f) -> p c f", c=DC),
                                     W1v[e, :, :, n * FW:(n + 1) * FW]).then_inc(s_raw[n % RAWS], 16)
                    else:
                        sp.dma_start(wview(r), W2v[e, :, JW * (n - FCH):JW * (n - FCH + 1), :]
                                     ).then_inc(s_raw[n % RAWS], 16)

            weights(0, 0)
            with sp.Fori(1, E) as t:
                weights(t, t)
            sp.wait_ge(s_route, 1)
            n_over = sp.value_load(over[0:1, 0:1], min_val=0, max_val=K_OVER)
            with sp.Fori(0, K_OVER) as s:
                e = sp.value_load(over[0:1, bass.ds(s + 1, 1)], min_val=0, max_val=E - 1)
                with sp.If(s < n_over):
                    weights(e, s + E)
            for c in range(C):
                sp.wait_ge(s_fin, c + 1)
                sp.dma_start(tok(out)[:, c, :], x2[:, c, :]).then_inc(s_out, 16)
            sp.wait_ge(s_out, 16 * C)

        @block.gpsimd
        def _(g):
            step = Count(g, s_pool)
            gp = nc.gpsimd
            gp.iota(iota16[:, :], pattern=[[1, 626]], base=0, channel_multiplier=0,
                    allow_small_or_imprecise_dtypes=True).then_inc(s_const, 1)
            step(gp.memset(ident[:, :], 0.0))
            gp.affine_select(out=ident[:, :], in_=ident[:, :], compare_op=ALU.not_equal, fill=1.0,
                             base=0, pattern=[[-1, 128]], channel_multiplier=1).then_inc(s_const, 1)
            step(gp.memset(identb[:, :], 0.0))
            gp.affine_select(out=identb[:, :], in_=identb[:, :], compare_op=ALU.not_equal, fill=1.0,
                             base=0, pattern=[[-1, 128]], channel_multiplier=1).then_inc(s_const, 1)
            for i, a in enumerate((gb1, gb2)):
                g.dma_start(bc[i][:, :], row(a).broadcast_to((P, D))).then_inc(s_bc, 16)
            gp.memset(onesb[:, :], 1.0).then_inc(s_const, 1)
            step(gp.memset(cmask[:, :], 0.0))
            gp.affine_select(out=cmask[:, :], in_=cmask[:, :], compare_op=ALU.is_ge, fill=-1e30,
                             base=0, pattern=[[-1, 126]], channel_multiplier=1).then_inc(s_const, 1)
            step(gp.memset(before[:, :], 1.0))
            gp.affine_select(out=before[:, :], in_=before[:, :], compare_op=ALU.is_gt, fill=0.0,
                             base=0, pattern=[[1, P]], channel_multiplier=-1).then_inc(s_const, 1)
            step(gp.memset(tri8[:, :, :], 1.0))
            gp.affine_select(out=tri8[:, :, :], in_=tri8[:, :, :], compare_op=ALU.is_ge, fill=0.0,
                             base=0, pattern=[[1, E], [-1, E]], channel_multiplier=0).then_inc(s_const, 1)
            gp.iota(iota8[:, :], pattern=[[1, E]], base=0, channel_multiplier=0,
                    allow_small_or_imprecise_dtypes=True).then_inc(s_const, 1)
            gp.iota(capk[:, :], pattern=[[CAP, K_OVER]], base=CAP, channel_multiplier=0,
                    allow_small_or_imprecise_dtypes=True).then_inc(s_const, 1)

            def add_counts(gr):
                g.wait_ge(s_cdec, gr + 1)
                gp.tensor_tensor(S[:, :, 0:HALF], S[:, :, 0:HALF], clo[:, :, :], ALU.add)
                gp.tensor_tensor(S[:, :, HALF:NP], S[:, :, HALF:NP], chi[:, :, :], ALU.add).then_inc(s_cadd, 1)

            for n in range(F_SLOTS):
                if n < len(GROUPS) - 1:
                    add_counts(n)
                g.wait_ge(s_fhi, n + 1)
                gp.tensor_tensor(wlo[n][:, :], raw[n % F_RAWS][:, :], whi[n][:, :], ALU.subtract).then_inc(s_flo0, 1)

            g.wait_ge(s_bc, 32)
            g.wait_ge(s_ln0, C)
            for c in range(C):
                gp.tensor_tensor(xs[:, c, :], xs[:, c, :], bc[1][:, :], ALU.add).then_inc(s_xb, 1)
            g.wait_ge(s_xb, C)
            g.dma_start(bc[1][:, :], row(bp).broadcast_to((P, D))).then_inc(s_bp, 16)

            g.wait_ge(s_bp, 16)
            for c in range(C):
                g.wait_ge(s_n1, c + 1)
                gp.tensor_tensor(xf[:, c, :], xf[:, c, :], bc[1][:, :], ALU.add).then_inc(s_xfb, 1)
            g.dma_start(tok(x1_d), xs[:, :, :]).then_inc(s_x1st, 16)
            g.wait_ge(s_xfb, C)
            g.dma_start(tok(xf_d), xf[:, :, :]).then_inc(s_xfst, 16)

            g.wait_ge(s_sc, UNITS)
            g.wait_ge(s_xfst, 16)
            g.wait_ge(s_x1st, 16)
            g.dma_start(x2[:, :, :], tok(xf_d)).then_inc(s_xfld, 16)
            g.dma_start(base[:, :, :], tok(x1_d)).then_inc(s_x1ld, 16)
            g.wait_ge(s_x1ld, 16)
            for c in range(C):
                g.wait_ge(s_x2, c + 1)
                gp.tensor_tensor(base[:, c, :], base[:, c, :], x2[:, c, :], ALU.add).then_inc(s_base, 1)

            g.wait_ge(s_zero, 16 * (TILES + 1 + K_OVER))
            g.wait_ge(s_slot, 1)
            g.wait_ge(s_n2, C)
            for c in range(C):
                g.indirect_dma_start(out=hs_d[:, :], out_offset=bass.IndirectOffsetOnAxis(ap=slot[:, c:c + 1], axis=0),
                                     in_=n2[:, c, :], in_offset=None).then_inc(s_scat, 16)
            g.wait_ge(s_scat, 16 * C)
            g.dma_start(hs[0:CAP, :], hs_d[0:CAP, :]).then_inc(s_hs, 16)

            g.wait_ge(s_base, C)
            for c in range(C):
                g.indirect_dma_start(out=x2[:, c, :], out_offset=None, in_=b2[:, :],
                                     in_offset=bass.IndirectOffsetOnAxis(ap=eidx[:, c:c + 1], axis=0)
                                     ).then_inc(s_b2g, 16)

            def tile(t):
                g.wait_ge(s_hgT, t + 1)
                g.dma_start(hs[0:CAP, :], hs_d[bass.ds((t + 1) * CAP, CAP), :]).then_inc(s_hs, 16)
                g.wait_ge(s_yev, 2 * t + 2)
                g.dma_start(ys_d[bass.ds(t * CAP, CAP), :], ysb[0:CAP, :]).then_inc(s_yst, 16)

            g.wait_ge(s_route, 1)
            n_over = g.value_load(over[0:1, 0:1], min_val=0, max_val=K_OVER)
            with g.Fori(0, E) as t:
                tile(t)
            with g.Fori(0, K_OVER) as s:
                with g.If(s < n_over):
                    tile(s + E)
            g.wait_ge(s_yev, 2 * (n_over + E) + 2)
            g.dma_start(ys_d[bass.ds((n_over + E) * CAP, CAP), :], ysb[0:CAP, :]).then_inc(s_ylast, 16)
            g.wait_ge(s_ylast, 16)
            g.wait_ge(s_base2, C)
            for c in range(C):
                g.indirect_dma_start(out=x2[:, c, :], out_offset=None, in_=ys_d[:, :],
                                     in_offset=bass.IndirectOffsetOnAxis(ap=slot1[:, c:c + 1], axis=0)
                                     ).then_inc(s_yg, 16)
            g.wait_ge(s_yg, 16 * C)

        @block.scalar
        def _(a):
            act = nc.scalar

            def hi(out_, in_, s, func=ACT.Copy):
                act.activation(out_, in_, func).then_inc(s, 1)

            roots = [0]

            def root_of(n=1):
                roots[0] += 1
                a.wait_ge(s_var, roots[0])
                act.activation(root[:, 0:n], var[:, 0:n], ACT.Sqrt).then_inc(s_root, 1)

            def front(n):
                if n >= F_SLOTS:
                    a.wait_ge(*USED[(n - F_SLOTS) // 2])
                a.wait_ge(s_raw[n % F_RAWS], raw_value(n))
                hi(whi[n % F_SLOTS][:, :], raw[n % F_RAWS][:, :], s_fhi)

            a.wait_ge(s_zt, 1)
            for t in range(TILES + 1):
                a.dma_start(hs_d[t * CAP:(t + 1) * CAP, :], R0["zero"][0:CAP, :]).then_inc(s_zero, 16)
            for t in range(E + 1, TILES + 1):
                a.dma_start(ys_d[t * CAP:(t + 1) * CAP, :], R0["zero"][0:CAP, :]).then_inc(s_zero, 16)

            for g in range(len(GROUPS)):
                a.wait_ge(s_ohused, EU * sum(GROUPS[:g + 1]))
                if g:
                    a.wait_ge(s_cdec, g)
                act.activation(cint[:, :, :], ps[0:P, 0:C, 0:HALF], ACT.Copy).then_inc(s_cint, 1)
                if g == 0:
                    front(0)
                    a.wait_ge(s_misc, 1)
                    act.activation(lnT[:, :], ps[:, 6, 0:4 * DC], ACT.Copy).then_inc(s_miscev, 1)
                    act.activation(b1T[:, :], ps[:, 6, 128:320], ACT.Copy).then_inc(s_miscev, 1)
                if g == 1:
                    front(1)
            for c in range(C):
                a.wait_ge(s_S, C)
                act.activation(Sd[0][:, c, :], S[:, c, :], ACT.Copy).then_inc(s_Shi, 1)
            root_of(C)
            root_of(C)
            for c in range(C):
                a.wait_ge(s_ln0, c + 1)
                hi(xn[0][:, c, :], tmp[:, c % 2, :], s_xnh)
            front(2)

            def agg(r):
                for m in range(DC):
                    a.wait_ge(s_agg, r * DC + m + 1)
                    if not r and not m:
                        a.wait_ge(s_Slo, C)
                        a.wait_ge(s_zero, 16 * (TILES + 1 + K_OVER))
                    hi(halves(ag[0][:, m, :]), two(2 * (m % 2)), s_aggh)

            agg(0)
            for c in range(C):
                a.wait_ge(s_t, c + 1)
                hi(xn[0][:, c, :], tmp[:, c % 2, :], s_hh)
            front(3)
            front(4)
            agg(1)

            for _ in range(2 * C):
                root_of()
            for c in range(C):
                a.wait_ge(s_n1T, c + 1)
                if c >= 2:
                    a.wait_ge(s_hTl, c - 1)
                for m in range(DC):
                    act.activation(aff[:, c % 2, m, :], blocks(2 * (c % 2), 128, DC, P)[:, m, :], ACT.Identity,
                                   scale=lnT[:, m:m + 1], bias=lnT[:, DC + m:DC + m + 1]).then_inc(s_aff, 1)
                a.wait_ge(s_aff, DC * (c + 1))
                hi(hT[0][:, :, c * P:(c + 1) * P], aff[:, c % 2, :, :], s_hTh)
                if c == 0:
                    front(5)
                    front(6)

            def project_pairs(r):
                for m in range(PAIRS):
                    a.wait_ge(s_pj, r * PAIRS + m + 1)
                    if not r and not m:
                        a.wait_ge(s_xfst, 16)
                    hi(halves((q, k_)[r][0][:, m, :]), two(2 * (m % 2)), s_pjh)

            project_pairs(0)
            front(7)
            front(8)
            project_pairs(1)
            front(9)
            front(10)
            for c in range(C):
                a.wait_ge(s_pj, 2 * PAIRS + c + 1)
                if not c:
                    a.wait_ge(s_x1st, 16)
                hi(v[0][:, c, :].rearrange("p (a b) -> p a b", a=2), wide(4 + 2 * (c % 2), P), s_pjh)
            front(11)

            def split_hi(n, t):
                if isinstance(t, int) and n < SLOTS:
                    a.wait_ge(*USED[WV if n == 0 else WP])
                else:
                    a.wait_ge(s_used, SCH * t + n + 1 - SLOTS)
                a.wait_ge(s_raw[n % RAWS], (SCH // RAWS * 16) * t + FULL[n % RAWS] + 16 * (n // RAWS + 1))
                hi(whi[n % SLOTS][:, :], raw[n % RAWS][:, :], s_mhi)

            def turned(u):
                h, c = divmod(u, C)
                a.wait_ge(s_tr, u + 1)
                if u == 0:
                    a.wait_ge(s_ptz, 1)
                elif c == 0 and h or c == 2 and h:
                    a.wait_ge(s_pv, 2 * h - 1 + c // 2)
                for place, b0, nb in turned_parts(u):
                    ins = act.activation(pT[0][:, b0:b0 + nb, c * P:(c + 1) * P], place, ACT.Copy)
                ins.then_inc(s_trh, 1)

            def head_out(h):
                r0 = 64 * (h % 2)
                a.wait_ge(s_pv, 2 * h + 2)
                hi(halves(q[0][r0:r0 + 64, h // 2, :]), ps[r0:r0 + 64, 6:8, 0:HALF], s_pvh)

            for i in range(UNITS + 5):
                if 3 <= i < UNITS + 3:
                    turned(i - 3)
                if i < UNITS:
                    c = i % C
                    n = (c + 1) * P + (c + 1) % 2
                    a.wait_ge(s_mx, i + 1)
                    if i >= 3:
                        a.wait_ge(s_tr, i - 2)
                    act.activation(pr[:, i % 3, 0:n], score_rows(i)[:, 0:n], ACT.Exp, bias=negmax[:, i % 2, :],
                                   scale=float(D) ** -0.5, accum_out=ssum[:, i % 2, :]).then_inc(s_ex, 1)
                if i >= 9 and (i - 9) % C == 0:
                    head_out((i - 9) // C)

            split_hi(0, 0)

            def h2_turned(c):
                a.wait_ge(s_n2T, c + 1)
                for m in range(DC):
                    act.activation(h2T[:, m, c * P:(c + 1) * P], blocks(0, 128, DC, P)[:, m, :], ACT.Identity,
                                   scale=lnT[:, 2 * DC + m:2 * DC + m + 1],
                                   bias=lnT[:, 3 * DC + m:3 * DC + m + 1]).then_inc(s_h2T, 1)

            for c in range(C):
                if c == C - 1:
                    split_hi(1, 0)
                root_of()
                if c >= 1:
                    h2_turned(c - 1)
            h2_turned(C - 1)
            split_hi(2, 0)
            a.wait_ge(s_oh8, 1)
            act.activation(rt[:, 7, 0:C], rt[:, 6, 0:C], ACT.Exp).then_inc(s_act, 1)

            def tile_in(n_in, n_a):
                a.wait_ge(s_hgT, n_in)
                for m in range(DC):
                    act.activation(hgf[:, m, :], blocks(6, 128, DC, CAP)[:, m, :], ACT.Identity,
                                   scale=lnT[:, 2 * DC + m:2 * DC + m + 1],
                                   bias=lnT[:, 3 * DC + m:3 * DC + m + 1]).then_inc(s_hga, 1)
                a.wait_ge(s_hga, n_a)
                hi(hg[0][:, :, :], hgf[:, :, :], s_hgh)

            tile_in(1, DC)

            def tile(t, first):
                for k in range(SCH):
                    if k == 0:
                        for n in range(3 if first else 0, 3):
                            split_hi(n, t)
                        if not first:
                            a.wait_ge(s_used, SCH * t)
                            a.wait_ge(s_yst, 16 * t)
                        act.activation(ysb[0:CAP, 0:HB], ps[0:CAP, 4, 0:HB], ACT.Copy).then_inc(s_yev, 1)
                    if k + AHEAD < SCH:
                        split_hi(k + AHEAD, t)
                    if 1 <= k <= FCH:
                        a.wait_ge(s_used, SCH * t + k)
                        if k >= 3:
                            a.wait_ge(s_hidT, FCH * t + k - 2)
                        act.activation(hid[0:CAP, (k - 1) % 2, :], ps[0:CAP, (k - 1) % 2, 0:FW], ACT.Copy
                                       ).then_inc(s_hidev, 1)
                    if 2 <= k <= FCH + 1:
                        a.wait_ge(s_bia, FCH * t + k - 1)
                        hi(hTT[0][:, JW * (k - 2):JW * (k - 1), :], bia[:, k % 2, :, :], s_hTh2, ACT.Relu)
                    if k == FCH + 2:
                        tile_in(t + 2, DC * t + 2 * DC)

            tile(0, True)
            with a.Fori(1, E) as t:
                tile(t, False)
            a.wait_ge(s_route, 1)
            n_over = a.value_load(over[0:1, 0:1], min_val=0, max_val=K_OVER)
            with a.Fori(0, K_OVER) as s:
                with a.If(s < n_over):
                    tile(s + E, False)
            a.wait_ge(s_used, SCH * (n_over + E))
            a.wait_ge(s_yst, 16 * (n_over + E))
            act.activation(ysb[0:CAP, 0:HB], ps[0:CAP, 4, 0:HB], ACT.Copy).then_inc(s_yev, 1)

        @block.vector
        def _(d):
            dve = nc.vector
            step = Count(d, s_vec)

            def lo(out_, in_, hi_, s, relu=False):
                if relu:
                    dve.scalar_tensor_tensor(out_, in_, 0.0, hi_, ALU.max, ALU.subtract).then_inc(s, 1)
                else:
                    dve.tensor_tensor(out_, in_, hi_, ALU.subtract).then_inc(s, 1)

            def front(n):
                d.wait_ge(s_fhi, n + 1)
                lo(wlo[n % F_SLOTS][:, :], raw[n % F_RAWS][:, :], whi[n % F_SLOTS][:, :], s_flo)

            def rsqrt(in_, by, op, out_, n):
                rsqrts[0] += 1
                dve.tensor_scalar(var[:, 0:n], in_, by, None, op).then_inc(s_var, 1)
                d.wait_ge(s_root, rsqrts[0])
                step(dve.reciprocal(root[:, 0:n], root[:, 0:n]))
                step(dve.tensor_tensor(newt[:, 0:n], root[:, 0:n], root[:, 0:n], ALU.mult))
                step(dve.tensor_tensor(newt[:, 0:n], newt[:, 0:n], var[:, 0:n], ALU.mult))
                step(dve.tensor_scalar(newt[:, 0:n], newt[:, 0:n], -0.5, 1.5, ALU.mult, ALU.add))
                step(dve.tensor_tensor(out_, newt[:, 0:n], root[:, 0:n], ALU.mult))

            rsqrts = [0]

            def norm(out_, in_):
                dve.bn_stats(stats[:, 0, 0, :], in_[:, 0:HB])
                step(dve.bn_stats(stats[:, 0, 1, :], in_[:, HB:D]))
                step(dve.bn_aggr(mv[:, :], stats[:, 0, :, :]))
                rsqrt(mv[:, 1:2], EPS, ALU.add, rstd[:, :], 1)
                return dve.tensor_scalar(out_, in_, mv[:, 0:1], rstd[:, :], ALU.subtract, ALU.mult)

            dve.memset(R0["zero"][:, :], 0.0).then_inc(s_zt, 1)
            dve.memset(S[:, :, :], 0.0)
            step(dve.memset(ps[:, 4:6, 0:HB], 0.0))
            d.wait_ge(s_edges, 32)
            step(dve.tensor_copy(ef[:, 0:2, :], ei[:, :, :]))
            step(dve.tensor_scalar(ef[:, 2, :], ef[:, 1, :], float(HALF), None, ALU.is_ge))
            step(dve.scalar_tensor_tensor(ef[:, 3, :], ef[:, 2, :], -float(HALF), ef[:, 1, :], ALU.mult, ALU.add))
            step(dve.tensor_scalar(ef[:, 2, :], ef[:, 2, :], float(RADIX - 1), 1.0, ALU.mult, ALU.add))

            def onehots(i, first):
                for j in range(EU):
                    at = bass.ds(i * EU + j, 1)
                    if not first:
                        d.wait_ge(s_ohused, EU * i + j - (EU - 1))
                    dve.tensor_scalar(ohs[:, j, :], iota16[:, :], ef[:, 0, at], None, ALU.is_equal)
                    dve.tensor_scalar(ohd[:, j, :], iota16[:, 0:HALF], ef[:, 3, at], ef[:, 2, at],
                                      ALU.is_equal, ALU.mult).then_inc(s_oh, 1)

            def decode(g):
                d.wait_ge(s_cint, g + 1)
                if g:
                    d.wait_ge(s_cadd, g)
                dve.tensor_scalar(clo[:, :, :], cint[:, :, :], RADIX - 1, None, ALU.bitwise_and)
                dve.tensor_scalar(chi[:, :, :], cint[:, :, :], 12, None, ALU.logical_shift_right).then_inc(s_cdec, 1)

            d.wait_ge(s_const, 9)
            dve.tensor_copy(onesr[:, :], onesb[:, 0:2]).then_inc(s_busy, 1)
            at = 0
            for g, steps in enumerate(GROUPS):
                if g == 0:
                    onehots(0, True)
                    with d.Fori(1, steps) as i:
                        onehots(i, False)
                else:
                    with d.Fori(at, at + steps) as i:
                        onehots(i, False)
                at += steps
                decode(g)
            d.wait_ge(s_cdec, len(GROUPS))
            dve.tensor_tensor(S[:, :, 0:HALF], S[:, :, 0:HALF], clo[:, :, :], ALU.add)
            step(dve.tensor_tensor(S[:, :, HALF:NP], S[:, :, HALF:NP], chi[:, :, :], ALU.add))
            for c in range(C):
                dve.tensor_tensor(S[:, c, c * P:(c + 1) * P], S[:, c, c * P:(c + 1) * P],
                                  ident[0:P, 0:P], ALU.add).then_inc(s_S, 1)
            for c in range(C):
                d.wait_ge(s_Shi, c + 1)
                lo(Sd[1][:, c, :], S[:, c, :], Sd[0][:, c, :], s_Slo)
            d.wait_ge(s_x, 16)
            for c in range(C):
                for i in range(2):
                    ins = dve.bn_stats(stats[:, c, i, :], xs[:, c, i * HB:(i + 1) * HB])
            step(ins)
            for c in range(C):
                ins = dve.bn_aggr(mvx[:, c, :], stats[:, c, :, :])
            step(ins)
            rsqrt(mvx[:, :, 1], EPS, ALU.add, rx[:, 0, :], C)
            d.wait_ge(s_deg, 1)
            deg = ps[0:P, 5, 0:2 * C].rearrange("p (c o) -> p c o", o=2)[:, :, 0]
            dve.tensor_scalar(dtmp[:, 0, :], deg, 0.0, None, ALU.is_gt)
            rsqrt(deg, 1.0, ALU.max, dtmp[:, 1, :], C)
            step(dve.tensor_tensor(dinv[:, :], dtmp[:, 0, :], dtmp[:, 1, :], ALU.mult))
            dve.tensor_tensor(rx[:, 1, :], rx[:, 0, :], dinv[:, :], ALU.mult).then_inc(s_dinv, 1)
            step(dve.reduce_max(mv[:, 0:1], deg, AX))
            dve.tensor_scalar(big[:, 0:1], mv[:, 0:1], float(BIG), None, ALU.is_ge).then_inc(s_big, 1)
            d.wait_ge(s_dinv, 1)

            for c in range(C + 1):
                if 2 <= c < C:
                    d.wait_ge(s_xnl, c - 1)
                if c < C:
                    dve.tensor_scalar(tmp[:, c % 2, :], xs[:, c, :], mvx[:, c, 0:1], rx[:, 1, c:c + 1],
                                      ALU.subtract, ALU.mult).then_inc(s_ln0, 1)
                if c:
                    d.wait_ge(s_xnh, c)
                    lo(xn[1][:, c - 1, :], tmp[:, (c - 1) % 2, :], xn[0][:, c - 1, :], s_xnl)
                if c == 1:
                    d.wait_ge(s_bigs, 1)
                    dve.tensor_copy(bigi[0:1, 0:1], ps[0:1, 4, 0:1]).then_inc(s_bigi, 1)

            def agg(r):
                for m in range(DC):
                    d.wait_ge(s_aggh, r * DC + m + 1)
                    lo(halves(ag[1][:, m, :]), two(2 * (m % 2)), halves(ag[0][:, m, :]), s_aggl)

            agg(0)
            d.wait_ge(s_bc, 32)
            for c in range(C):
                d.wait_ge(s_xw, c + 1)
                if c >= 2:
                    d.wait_ge(s_hl, c - 1)
                dve.scalar_tensor_tensor(tmp[:, c % 2, :].rearrange("p (a b) -> p a b", a=2), wide(4 + 2 * (c % 2), P),
                                         dinv[:, c:c + 1], bc[0][:, :].rearrange("p (a b) -> p a b", a=2),
                                         ALU.mult, ALU.add).then_inc(s_tb, 1)
                d.wait_ge(s_tb, c + 1)
                dve.tensor_scalar(tmp[:, c % 2, :], tmp[:, c % 2, :], 0.0, dinv[:, c:c + 1], ALU.max, ALU.mult
                                  ).then_inc(s_t, 1)
                d.wait_ge(s_hh, c + 1)
                lo(xn[1][:, c, :], tmp[:, c % 2, :], xn[0][:, c, :], s_hl)
            front(3)
            front(4)
            agg(1)
            d.wait_ge(s_xb, C)
            for c in range(C):
                d.wait_ge(s_xw, C + c + 1)
                dve.scalar_tensor_tensor(xs[:, c, :].rearrange("p (a b) -> p a b", a=2), wide(4 + 2 * (c % 2), P),
                                         dinv[:, c:c + 1], xs[:, c, :].rearrange("p (a b) -> p a b", a=2),
                                         ALU.mult, ALU.add).then_inc(s_x1, 1)
                d.wait_ge(s_x1, c + 1)
                norm(xf[:, c, :], xs[:, c, :]).then_inc(s_xf, 1)
                d.wait_ge(s_xf, c + 1)
                norm(n1[:, c, :], xf[:, c, :]).then_inc(s_n1, 1)
            for c in range(C):
                rows_ = slice(c * P, (c + 1) * P)
                d.wait_ge(s_hTh, c + 1)
                lo(hT[1][:, :, rows_], aff[:, c % 2, :, :], hT[0][:, :, rows_], s_hTl)
                if c == 0:
                    front(5)
                    front(6)
            for i in range(2):
                dve.memset(hT[i][:, :, N:NP].bitcast(F32), 0.0).then_inc(s_pad, 1)

            def project_pairs(r):
                for m in range(PAIRS):
                    d.wait_ge(s_pjh, r * PAIRS + m + 1)
                    lo(halves((q, k_)[r][1][:, m, :]), two(2 * (m % 2)), halves((q, k_)[r][0][:, m, :]), s_pjl)

            project_pairs(0)
            front(7)
            front(8)
            project_pairs(1)
            front(9)
            front(10)
            for c in range(C):
                d.wait_ge(s_pjh, 2 * PAIRS + c + 1)
                lo(v[1][:, c, :].rearrange("p (a b) -> p a b", a=2), wide(4 + 2 * (c % 2), P),
                   v[0][:, c, :].rearrange("p (a b) -> p a b", a=2), s_pjl)
            front(11)
            d.wait_ge(s_pj, 2 * PAIRS + C)
            for i in range(2):
                for b in range(1, C, 2):
                    dve.memset(pT[i][:, b, b * P - 1:b * P].bitcast(F32), 0.0)
                last = dve.memset(pT[i][:, :, N:NP].bitcast(F32), 0.0)
            last.then_inc(s_ptz, 1)

            def turned(u):
                c = u % C
                d.wait_ge(s_trh, u + 1)
                cols = slice(c * P, (c + 1) * P)
                for place, b0, nb in turned_parts(u):
                    ins = dve.tensor_tensor(pT[1][:, b0:b0 + nb, cols], place,
                                            pT[0][:, b0:b0 + nb, cols], ALU.subtract)
                ins.then_inc(s_trl, 1)

            def head_out(h):
                r0 = 64 * (h % 2)
                d.wait_ge(s_pvh, h + 1)
                lo(halves(q[1][r0:r0 + 64, h // 2, :]), ps[r0:r0 + 64, 6:8, 0:HALF],
                   halves(q[0][r0:r0 + 64, h // 2, :]), s_pvl)

            for i in range(UNITS + 5):
                if i < UNITS:
                    c = i % C
                    n = (c + 1) * P + (c + 1) % 2
                    d.wait_ge(s_sc, i + 1)
                    dve.reduce_max(smax[:, i % 2, :], score_rows(i)[:, 0:n], AX).then_inc(s_rmx, 1)
                if 1 <= i <= UNITS:
                    d.wait_ge(s_ex, i)
                    dve.reciprocal(rsum[:, i % 2, :], ssum[:, (i - 1) % 2, :]).then_inc(s_rs, 1)
                if i < UNITS:
                    d.wait_ge(s_rmx, i + 1)
                    dve.tensor_scalar(negmax[:, i % 2, :], smax[:, i % 2, :], -(float(D) ** -0.5), None,
                                      ALU.mult).then_inc(s_mx, 1)
                if 3 <= i < UNITS + 3:
                    turned(i - 3)
                if 1 <= i <= UNITS:
                    d.wait_ge(s_rs, i)
                    n = ((i - 1) % C + 1) * P
                    dve.tensor_scalar(pr[:, (i - 1) % 3, 0:n], pr[:, (i - 1) % 3, 0:n], rsum[:, i % 2, :], None,
                                      ALU.mult).then_inc(s_nm, 1)
                if i >= 9 and (i - 9) % C == 0:
                    head_out((i - 9) // C)
            d.wait_ge(s_pv, 2 * H)

            def split_lo(n, t):
                d.wait_ge(s_mhi, SCH * t + n + 1)
                lo(wlo[n % SLOTS][:, :], raw[n % RAWS][:, :], whi[n % SLOTS][:, :], s_mlo)

            d.wait_ge(s_xfld, 16)
            split_lo(0, 0)
            for c in range(C):
                d.wait_ge(s_wp, c + 1)
                dve.tensor_tensor(x2[:, c, :].rearrange("p (a b) -> p a b", a=2), wide(4 + 2 * (c % 2), P),
                                  x2[:, c, :].rearrange("p (a b) -> p a b", a=2), ALU.add).then_inc(s_x2, 1)
                d.wait_ge(s_x2, c + 1)
                norm(n2[:, c, :], x2[:, c, :]).then_inc(s_n2, 1)
            split_lo(1, 0)

            d.wait_ge(s_gate, 1)
            lg = rt[:, 0, 0:C * E].rearrange("p (c e) -> p c e", e=E)
            mx8 = rt[:, 1, 0:C * E].rearrange("p (c e) -> p c e", e=E)
            ix8 = rt[:, 2, 0:C * E].rearrange("p (c e) -> p c e", e=E).bitcast(U32)
            ohe = rt[:, 3, 0:C * E].rearrange("p (c e) -> p c e", e=E)
            ef5 = rt[:, 6, 8:8 + C]
            step(dve.tensor_copy(lg, ps[0:P, 2, 0:C * E].rearrange("p (c e) -> p c e", e=E)))
            for c in range(C):
                last = dve.max(mx8[:, c, :], lg[:, c, :])
            step(last)
            for c in range(C):
                last = dve.max_index(ix8[:, c, :], mx8[:, c, :], lg[:, c, :])
            step(last)
            dve.tensor_tensor(rt[:, 6, 0:C], mx8[:, :, 0], mx8[:, :, 0], ALU.subtract)
            dve.tensor_copy(eidx[:, :], ix8[:, :, 0])
            step(dve.tensor_copy(ef5, ix8[:, :, 0]))
            for c in range(C):
                last = dve.tensor_scalar(ohe[:, c, :], iota8[:, :], ef5[:, c:c + 1], None, ALU.is_equal)
            step(last)
            ohb = rt[:, 4, 0:C * E // 2].bitcast(BF16).rearrange("p (c e) -> p c e", e=E)
            dve.tensor_copy(ohb, ohe).then_inc(s_oh8, 1)
            d.wait_ge(s_act, 1)
            step(dve.reciprocal(rt[:, 7, 8:8 + C], rt[:, 7, 0:C]))
            dve.tensor_tensor(wtok[:, :], rt[:, 7, 0:C], rt[:, 7, 8:8 + C], ALU.mult)
            split_lo(2, 0)
            d.wait_ge(s_rank, 1)
            rank8 = ps[0:P, 3, 0:C * E].rearrange("p (c e) -> p c e", e=E)
            cnt = ps[0:P, 3, C * E:C * E + E]
            nov = rt[:, 5, 0:8]
            ovend = rt[:, 5, 8:16]
            ovb = rt[:, 5, 16:24]
            rank = rt[:, 5, 24:24 + C]
            qt = rt[:, 5, 32:32 + C]
            sl = rt[:, 5, 40:40 + C]
            kk = rt[:, 6, 16:16 + C]
            tk = rt[:, 8, 0:E * K_OVER].rearrange("p (e k) -> p e k", k=K_OVER)
            rk = rt[:, 9, 0:C * K_OVER].rearrange("p (c k) -> p c k", k=K_OVER)
            ok = rt[0:1, 4, 0:E * K_OVER].rearrange("p (s e) -> p s e", e=E)
            prod = rt[:, 0, 0:C * E].rearrange("p (c e) -> p c e", e=E)
            step(dve.tensor_tensor(prod, rank8, ohe, ALU.mult))
            step(dve.reduce_sum(rank, prod, AX))
            dve.tensor_tensor(tk, cnt.rearrange("p (e o) -> p e o", o=1).broadcast_to((P, E, K_OVER)),
                              capk[:, :].rearrange("p (o k) -> p o k", o=1).broadcast_to((P, E, K_OVER)), ALU.is_gt)
            step(dve.tensor_tensor(rk, rank.rearrange("p (c o) -> p c o", o=1).broadcast_to((P, C, K_OVER)),
                                   capk[:, :].rearrange("p (o k) -> p o k", o=1).broadcast_to((P, C, K_OVER)),
                                   ALU.is_ge))
            dve.reduce_sum(nov, tk, AX)
            step(dve.reduce_sum(qt, rk, AX))
            step(dve.tensor_tensor(tp[:, :, :], tri8[:, :, :],
                                   nov.rearrange("p (o e) -> p o e", o=1).broadcast_to((P, E, E)), ALU.mult))
            step(dve.reduce_sum(ovend, tp[:, :, :], AX))
            dve.tensor_scalar(sl, qt, 0.0, None, ALU.is_gt)
            step(dve.tensor_tensor(ovb, ovend, nov, ALU.subtract))
            step(dve.tensor_tensor(prod, ohe, ovb.rearrange("p (o e) -> p o e", o=1).broadcast_to((P, C, E)), ALU.mult))
            step(dve.reduce_sum(kk, prod, AX))
            step(dve.tensor_tensor(kk, kk, qt, ALU.add))
            step(dve.scalar_tensor_tensor(kk, kk, float(E - 1), ef5, ALU.add, ALU.subtract))
            step(dve.tensor_tensor(kk, kk, sl, ALU.mult))
            step(dve.tensor_tensor(kk, kk, ef5, ALU.add))
            step(dve.tensor_tensor(kk, kk, qt, ALU.subtract))
            step(dve.scalar_tensor_tensor(sl, kk, float(CAP), rank, ALU.mult, ALU.add))
            dve.tensor_copy(slot[:, :], sl).then_inc(s_slot, 1)
            dve.tensor_scalar(slot1[:, :], sl, float(CAP), None, ALU.add)
            dve.tensor_copy(over[0:1, 0:1], ovend[0:1, E - 1:E])
            step(dve.tensor_tensor(ok, ovend[0:1, :].rearrange("p (o e) -> p o e", o=1).broadcast_to((1, K_OVER, E)),
                                   iota8[0:1, 0:K_OVER].rearrange("p (s o) -> p s o", o=1).broadcast_to((1, K_OVER, E)),
                                   ALU.is_le))
            step(dve.reduce_sum(rt[0:1, 6, 32:32 + K_OVER], ok, AX))
            step(dve.tensor_scalar(rt[0:1, 6, 32:32 + K_OVER], rt[0:1, 6, 32:32 + K_OVER], float(E - 1), None, ALU.min))
            dve.tensor_copy(over[0:1, 1:1 + K_OVER], rt[0:1, 6, 32:32 + K_OVER]).then_inc(s_route, 1)

            def tile_in(n_h):
                d.wait_ge(s_hgh, n_h)
                lo(hg[1][:, :, :], hgf[:, :, :], hg[0][:, :, :], s_hgl)

            tile_in(1)
            for c in range(C):
                d.wait_ge(s_b2g, 16 * C)
                d.wait_ge(s_base, C)
                dve.scalar_tensor_tensor(base[:, c, :], x2[:, c, :], wtok[:, c:c + 1], base[:, c, :],
                                         ALU.mult, ALU.add).then_inc(s_base2, 1)


            def tile(e, t, first):
                for k in range(SCH):
                    if k == 0:
                        for n in range(2 if first else 0, 2):
                            split_lo(n, t)
                        if not first:
                            d.wait_ge(s_used, SCH * t)
                            d.wait_ge(s_yst, 16 * t)
                        dve.tensor_copy(ysb[0:CAP, HB:D], ps[0:CAP, 5, 0:HB]).then_inc(s_yev, 1)
                    if 2 <= k <= FCH + 1:
                        d.wait_ge(s_hidT, FCH * t + k - 1)
                        bcol = b1T[:, bass.ds(e * (DF // 128) + JW * (k - 2), JW)]
                        dve.tensor_tensor(bia[:, k % 2, :, :], blocks(2 + k % 2, 128, JW, CAP),
                                          bcol.rearrange("p (j o) -> p j o", o=1).broadcast_to((128, JW, CAP)),
                                          ALU.add).then_inc(s_bia, 1)
                    if k + 2 < SCH and not (first and k == 0):
                        split_lo(k + 2, t)
                    if 2 <= k <= FCH + 1:
                        d.wait_ge(s_hTh2, FCH * t + k - 1)
                        lo(hTT[1][:, JW * (k - 2):JW * (k - 1), :], bia[:, k % 2, :, :],
                           hTT[0][:, JW * (k - 2):JW * (k - 1), :], s_hTl2, relu=True)
                    if k == FCH + 2:
                        tile_in(t + 2)

            tile(0, 0, True)
            with d.Fori(1, E) as t:
                tile(t, t, False)
            d.wait_ge(s_route, 1)
            n_over = d.value_load(over[0:1, 0:1], min_val=0, max_val=K_OVER)
            with d.Fori(0, K_OVER) as s:
                e = d.value_load(over[0:1, bass.ds(s + 1, 1)], min_val=0, max_val=E - 1)
                with d.If(s < n_over):
                    tile(e, s + E, False)
            d.wait_ge(s_used, SCH * (n_over + E))
            d.wait_ge(s_yst, 16 * (n_over + E))
            dve.tensor_copy(ysb[0:CAP, HB:D], ps[0:CAP, 5, 0:HB]).then_inc(s_yev, 1)
            for c in range(C):
                d.wait_ge(s_yg, 16 * C)
                dve.scalar_tensor_tensor(x2[:, c, :], x2[:, c, :], wtok[:, c:c + 1], base[:, c, :],
                                         ALU.mult, ALU.add).then_inc(s_fin, 1)

        @block.tensor
        def _(pe):
            mm = nc.tensor.matmul

            def wpart(n, c):
                i = (n + c // 3) % F_SLOTS
                return wview(whi[i])[:, c % 3, :], wview(wlo[i])[:, c % 3, :]

            def count(i, first, last):
                for j in range(EU):
                    pe.wait_ge(s_oh, EU * i + j + 1)
                    for m in range(C):
                        ins = mm(ps[0:P, m, 0:HALF], ohs[:, j, m * P:(m + 1) * P], ohd[:, j, :],
                                 start=first and j == 0, stop=last and j == EU - 1)
                    ins.then_inc(s_ohused, 1)

            at = 0
            for g, steps in enumerate(GROUPS):
                if g:
                    pe.wait_ge(s_cint, g)
                count(at, True, False)
                with pe.Fori(at + 1, at + steps - 1) as i:
                    count(i, False, False)
                count(at + steps - 1, False, True)
                at += steps
                if g == 0:
                    pe.wait_ge(s_const, 9)
                    pe.wait_ge(s_rows, 64)
                    pe.wait_ge(s_b1r, 32)
                    nc.tensor.transpose(ps[:, 6, 0:4 * DC], rows[:, :], ident[0:4 * DC, 0:4 * DC])
                    for i in range(2):
                        ins = nc.tensor.transpose(ps[:, 6, 128 + 96 * i:224 + 96 * i], b1r[:, i, :], ident[0:96, 0:96])
                    ins.then_inc(s_misc, 1)

            def keep_busy(n, left, right):
                for _ in range(n):
                    mm(ps[0:left.shape[-1], 7, 0:512], left, right, start=True, stop=True)

            keep_busy(DECODE_BUSY, onesb[:, :], ohs[:, 0, 0:512])
            pe.wait_ge(s_busy, 1)
            pe.wait_ge(s_Shi, C)
            pe.wait_ge(s_Slo, C)
            for c2 in range(C):
                for c in range(C):
                    for i, t in enumerate(Sd):
                        ins = mm(ps[0:P, 5, 2 * c2:2 * c2 + 2], t[:, c, c2 * P:(c2 + 1) * P], onesr[:, :],
                                 start=c == 0 and i == 0, stop=c == C - 1 and i == 1)
            ins.then_inc(s_deg, 1)
            keep_busy(DEG_BUSY, onesb[:, :], ohs[:, 0, 0:512])
            pe.wait_ge(s_big, 1)
            mm(ps[0:1, 4, 0:2], big[:, 0:1], onesb[:, 0:2], start=True, stop=True).then_inc(s_bigs, 1)
            keep_busy(DEG_BUSY, onesb[:, :], ohs[:, 0, 0:512])
            pe.wait_ge(s_bigi, 1)
            any_big = pe.value_load(bigi[0:1, 0:1], min_val=0, max_val=P)

            def aggregate(r, exact):
                for m in range(DC):
                    if r or m >= 2:
                        pe.wait_ge(s_aggl, r * DC + m - 1)
                    for half in range(2):
                        for c in range(C):
                            if not r and not m and not half:
                                pe.wait_ge(s_xnl, c + 1)
                            xp = [t[:, c, m * 128:(m + 1) * 128] for t in xn]
                            sp_ = [t[:, c, half * HALF:(half + 1) * HALF] for t in Sd]
                            products = pairs(sp_, xp)[0:2 if exact else 3]
                            for i, (rr, l) in enumerate(products):
                                ins = mm(ps[:, 2 * (m % 2) + half, 0:HALF], l, rr, start=c == 0 and i == 0,
                                         stop=c == C - 1 and i == len(products) - 1)
                    ins.then_inc(s_agg, 1)

            def aggregation(r):
                with pe.If(any_big > 0):
                    aggregate(r, False)
                with pe.If(any_big < 1):
                    aggregate(r, True)

            def rows_product(lhs, n, c, bank):
                for half in range(2):
                    for m in range(DC):
                        lp = [t[:, m, c * P:(c + 1) * P] for t in lhs]
                        wp = [t[:, half * HB:(half + 1) * HB] for t in wpart(n, m)]
                        for i, (l, rr) in enumerate(pairs(lp, wp)):
                            ins = mm(ps[0:P, bank + half, 0:HB], l, rr,
                                     start=m == 0 and i == 0, stop=m == DC - 1 and i == 2)
                return ins

            pe.wait_ge(s_miscev, 2)
            aggregation(0)
            pe.wait_ge(s_aggl, DC)
            pe.wait_ge(*split(2))
            for c in range(C):
                if c >= 2:
                    pe.wait_ge(s_t, c - 1)
                ins = rows_product(ag, 2 * GNN1, c, 4 + 2 * (c % 2))
                ins.then_inc(s_xw, 1)
            pe.wait_ge(s_hl, C)
            aggregation(1)
            pe.wait_ge(s_aggl, 2 * DC)
            pe.wait_ge(*split(4))
            for c in range(C):
                pe.wait_ge(s_x1, c - 1) if c >= 2 else pe.wait_ge(s_t, C)
                rows_product(ag, 2 * GNN2, c, 4 + 2 * (c % 2)).then_inc(s_xw, 1)
            for c in range(C):
                pe.wait_ge(s_n1, c + 1)
                if c >= 2:
                    pe.wait_ge(s_aff, DC * (c - 1))
                for m in range(DC):
                    ins = nc.tensor.transpose(blocks(2 * (c % 2), 128, DC, P)[:, m, :], n1[:, c, m * 128:(m + 1) * 128],
                                              ident[0:P, 0:P])
                ins.then_inc(s_n1T, 1)

            pe.wait_ge(s_hTl, C)
            pe.wait_ge(s_pad, 2)
            for r, w in enumerate((WQ, WK)):
                pe.wait_ge(*split(2 * w + 2))
                for m in range(PAIRS):
                    if r or m >= 2:
                        pe.wait_ge(s_pjl, r * PAIRS + m - 1)
                    for half in range(2):
                        for c in range(DC):
                            wp = [t[:, m * 128:(m + 1) * 128] for t in wpart(2 * w, c)]
                            hp = [t[:, c, half * HALF:(half + 1) * HALF] for t in hT]
                            for i, (l, rr) in enumerate(pairs(wp, hp)):
                                ins = mm(ps[:, 2 * (m % 2) + half, 0:HALF], l, rr,
                                         start=c == 0 and i == 0, stop=c == DC - 1 and i == 2)
                    ins.then_inc(s_pj, 1)
            pe.wait_ge(*split(2 * WV + 2))
            for c in range(C):
                if c >= 2:
                    pe.wait_ge(s_pjl, 2 * PAIRS + c - 1)
                rows_product(hT, 2 * WV, c, 4 + 2 * (c % 2)).then_inc(s_pj, 1)
            pe.wait_ge(s_pjl, 2 * PAIRS + C)

            def scores(u):
                h, c = divmod(u, C)
                r0, m = 64 * (h % 2), h // 2
                n = (c + 1) * P + (c + 1) % 2
                if u >= 3:
                    pe.wait_ge(s_ex, u - 2)
                b = score_banks(u)
                for a0, a1 in ((0, min(n, 512)), (512, n)):
                    if a1 <= a0:
                        continue
                    bank = b + a0 // 512
                    qp = [t[r0:r0 + 64, m, c * P:(c + 1) * P] for t in q]
                    kp = [t[r0:r0 + 64, m, a0:a1] for t in k_]
                    d0, d1 = max(c * P, a0), min(n, a1)
                    for i, (l, rr) in enumerate(pairs(qp, kp)):
                        ins = mm(ps[0:P, bank, 0:a1 - a0], l, rr, start=i == 0, stop=i == 2)
                        if i == 0 and d1 > d0:
                            mm(ps[0:P, bank, d0 - a0:d1 - a0], identb[0:P, 0:P], cmask[:, d0 - c * P:d1 - c * P],
                               start=False, stop=False)
                ins.then_inc(s_sc, 1)

            def turn(u):
                pe.wait_ge(s_nm, u + 1)
                if u >= 2:
                    pe.wait_ge(s_trl, u - 1)
                for place, b0, nb in turned_parts(u):
                    for b in range(nb):
                        ins = nc.tensor.transpose(place[:, b, :],
                                                  pr[:, u % 3, (b0 + b) * P:(b0 + b + 1) * P], ident[0:P, 0:P])
                ins.then_inc(s_tr, 1)

            def values(h, half):
                m = h // 2
                pe.wait_ge(s_trl, C * h + (C if half else 3))
                if h:
                    pe.wait_ge(s_pvl, h)
                parts = []
                for b in range(C):
                    t0 = max(b * P - b % 2, half * HALF)
                    t1 = (half + 1) * HALF
                    if t0 < t1:
                        vp = [t[:, b, m * 128:(m + 1) * 128] for t in v]
                        pp = [t[:, b, t0:t1] for t in pT]
                        parts += [(t0, l, rr) for l, rr in pairs(vp, pp)]
                parts = parts[0:2] + parts[3:] + parts[2:3]
                for i, (t0, l, rr) in enumerate(parts):
                    ins = mm(ps[:, 6 + half, t0 - half * HALF:HALF], l, rr, start=i == 0, stop=i == len(parts) - 1)
                ins.then_inc(s_pv, 1)

            scores(0)
            for i in range(UNITS + 4):
                if i + 1 < UNITS:
                    scores(i + 1)
                    if i < 4:
                        keep_busy(4, k_[0][:, 0, 0:128], k_[0][:, 0, 0:512])
                if i >= 6 and (i - 6) % C == 0:
                    values((i - 6) // C, 0)
                if 2 <= i < UNITS + 2:
                    turn(i - 2)
                if i >= 8 and (i - 8) % C == 0:
                    values((i - 8) // C, 1)

            pe.wait_ge(s_pvl, H)
            pe.wait_ge(*split(FRONT))
            def turn_n2(c):
                pe.wait_ge(s_n2, c + 1)
                if c:
                    pe.wait_ge(s_h2T, DC * c)
                for m in range(DC):
                    ins = nc.tensor.transpose(blocks(0, 128, DC, P)[:, m, :], n2[:, c, m * 128:(m + 1) * 128],
                                              ident[0:P, 0:P])
                ins.then_inc(s_n2T, 1)

            def gate_products(c):
                pe.wait_ge(s_h2T, DC * (c + 1))
                for m in range(DC):
                    ins = mm(ps[0:P, 2, c * E:(c + 1) * E], h2T[:, m, c * P:(c + 1) * P], wg[:, m, :],
                             start=m == 0, stop=m == DC - 1)
                return ins

            pe.wait_ge(s_wg, 16)
            for c in range(C):
                if c >= 2:
                    pe.wait_ge(s_x2, c - 1)
                rows_product(q, 2 * WP, c, 4 + 2 * (c % 2)).then_inc(s_wp, 1)
                if c >= 2:
                    gate_products(c - 2)
                if c >= 1:
                    turn_n2(c - 1)
            gate_products(C - 2)
            turn_n2(C - 1)
            gate_products(C - 1).then_inc(s_gate, 1)
            pe.wait_ge(s_oh8, 1)
            ohb = rt[:, 4, 0:C * E // 2].bitcast(BF16).rearrange("p (c e) -> p c e", e=E)
            for c in range(C):
                for b in range(c + 1):
                    mm(ps[0:P, 3, c * E:(c + 1) * E], before[:, :] if b == c else onesb[:, :], ohb[:, b, :],
                       start=b == 0, stop=b == c)
            for b in range(C):
                ins = mm(ps[0:P, 3, C * E:(C + 1) * E], onesb[:, :], ohb[:, b, :], start=b == 0, stop=b == C - 1)
            ins.then_inc(s_rank, 1)

            def tile_in(n_in, n_read):
                pe.wait_ge(s_hs, n_in)
                if n_read is not None:
                    pe.wait_ge(s_hgl, n_read)
                for m in range(DC):
                    ins = nc.tensor.transpose(blocks(6, 128, DC, CAP)[:, m, :], hs[0:CAP, m * 128:(m + 1) * 128],
                                              ident[0:CAP, 0:CAP])
                ins.then_inc(s_hgT, 1)

            pe.wait_ge(s_route, 1)
            tile_in(16, None)

            def tile(t):
                first = isinstance(t, int)
                pe.wait_ge(s_hgl, t + 1)

                def turn_hid(k):
                    pe.wait_ge(s_hidev, FCH * t + k + 1)
                    if not first or k >= 2:
                        pe.wait_ge(s_bia, FCH * t + k - 1)
                    for j in range(JW):
                        ins = nc.tensor.transpose(blocks(2 + k % 2, 128, JW, CAP)[:, j, :],
                                                  hid[0:CAP, k % 2, j * 128:(j + 1) * 128], ident[0:CAP, 0:CAP])
                    ins.then_inc(s_hidT, 1)

                for k in range(FCH):
                    pe.wait_ge(s_mlo, SCH * t + k + 1)
                    if not first or k >= 2:
                        pe.wait_ge(s_hidev, FCH * t + k - 1)
                    i = k % SLOTS
                    for m in range(DC):
                        wp = [w[i][:, m * FW:(m + 1) * FW] for w in (whi, wlo)]
                        lp = [g_[:, m, :] for g_ in hg]
                        for j, (l, rr) in enumerate(pairs(lp, wp)):
                            ins = mm(ps[0:CAP, k % 2, 0:FW], l, rr, start=m == 0 and j == 0, stop=m == DC - 1 and j == 2)
                    ins.then_inc(s_used, 1)
                    if k:
                        turn_hid(k - 1)
                pe.wait_ge(s_yev, 2 * t + 2)
                for k in range(FCH):
                    pe.wait_ge(s_mlo, SCH * t + FCH + k + 1)
                    pe.wait_ge(s_hTl2, FCH * t + k + 1)
                    i = (FCH + k) % SLOTS
                    for half in range(2):
                        for j in range(JW):
                            wp = [w_[:, j, half * HB:(half + 1) * HB] for w_ in (wview(whi[i]), wview(wlo[i]))]
                            lp = [h_[:, JW * k + j, :] for h_ in hTT]
                            for jj, (l, rr) in enumerate(pairs(lp, wp)):
                                ins = mm(ps[0:CAP, 4 + half, 0:HB], l, rr, start=k == 0 and j == 0 and jj == 0,
                                         stop=k == FCH - 1 and j == JW - 1 and jj == 2)
                    ins.then_inc(s_used, 1)
                    if k == 0:
                        turn_hid(FCH - 1)
                    if k == 1:
                        tile_in(16 * t + 32, t + 1)

            tile(0)
            with pe.Fori(1, E) as t:
                tile(t)
            n_over = pe.value_load(over[0:1, 0:1], min_val=0, max_val=K_OVER)
            with pe.Fori(0, K_OVER) as s:
                with pe.If(s < n_over):
                    tile(s + E)


_INS = ["x", "src", "dst", "L0_gnn_W1", "L0_gnn_b1", "L0_gnn_W2", "L0_gnn_b2", "L0_ffn_ln1_g", "L0_ffn_ln1_b",
        "L0_ffn_ln2_g", "L0_ffn_ln2_b", "L0_ffn_Wq", "L0_ffn_Wk", "L0_ffn_Wv", "L0_ffn_Wp", "L0_ffn_bp",
        "L0_ffn_Wg", "L0_ffn_W1", "L0_ffn_b1", "L0_ffn_W2", "L0_ffn_b2"]


def kernel(**inputs):
    import numpy as _np
    import concourse.bacc as _bacc
    from concourse import mybir as _mybir
    from concourse.bass_utils import run_bass_kernel_spmd as _run

    nc = _bacc.Bacc("TRN2", target_bir_lowering=False, num_devices=1)
    arrays, args = {}, []
    for name in _INS:
        a = _np.ascontiguousarray(inputs[name])
        arrays[f"in_{name}"] = a
        args.append(nc.dram_tensor(f"in_{name}", a.shape, _mybir.dt.from_np(a.dtype), kind="ExternalInput").ap())
    out = nc.dram_tensor("out_x", (N, D), F32, kind="ExternalOutput").ap()
    build(nc, *args, out)
    r = _run(nc, [arrays], core_ids=[0])
    return r.results[0]["out_x"]
```

```python
from contextlib import ExitStack

import concourse.bass as bass
from concourse import mybir

F32 = mybir.dt.float32
F32R = mybir.dt.float32r
BF16 = mybir.dt.bfloat16
F16 = mybir.dt.float16
I32 = mybir.dt.int32
U32 = mybir.dt.uint32
ALU = mybir.AluOpType
ACT = mybir.ActivationFunctionType
AX = mybir.AxisListType.X

N, D = 625, 768
NE = 10000
H, HS = 12, 64
E, DF = 8, 3072
EPS = 1e-5

P = 125
C = N // P
HALF = 314
NP = 2 * HALF
DC = D // 128
HB = D // 2
PAIRS = H // 2

BIG = 4096
EC = NE // P
EU = 4
GROUPS = [8, 8, EC // EU - 16]
RADIX = 4096

CAP = 128
K_OVER = N // CAP
TILES = E + K_OVER

CH = 3 * D
FCH = DF // (CH // DC)
FW = CH // DC
JW = FW // 128
SCH = 2 * FCH
AHEAD = 3
SLOTS = 4
RAWS = 4
GNN1, GNN2, WV, WQ, WK, WP = range(6)
FRONT = 12
PAIR_FRONT = {(0, 1): 8, (0, 3): 9, (1, 1): 10}
F_SLOTS, F_RAWS = 3, 2
F_SLOT = (0, 1, 2, 0, 1, 2, 0, 3, 1, 2, 0, 1)
E_SLOT = 2

DECODE_BUSY = 66
DEG_BUSY = 10
ROW_BUSY = 3
HIDDEN_BUSY = 8
FILL_BUSY = 8
DRAIN_BUSY = 3
TURN_BUSY = 24
LOAD_BUSY = 20


def pairs(hi_lo_a, hi_lo_b):
    (ah, al), (bh, bl) = hi_lo_a, hi_lo_b
    return ((ah, bh), (ah, bl), (al, bh))


def build(nc, x, src, dst, gW1, gb1, gW2, gb2, ln1_g, ln1_b, ln2_g, ln2_b,
          Wq, Wk, Wv, Wp, bp, Wg, W1, b1, W2, b2, out):
    ctx = ExitStack()
    with ctx:
        def sb(name, shape, dt, stack=ctx):
            return stack.enter_context(nc.sbuf_tensor(name, shape, dt))

        def sem(name):
            return ctx.enter_context(nc.semaphore(name))

        def region(name, size, *variants):
            made = {}
            for variant in variants:
                with ExitStack() as s:
                    for n, shape, dt in variant:
                        made[n] = sb(n, shape, dt, s)
            sb(name, [128, size], F32)
            return made

        x1_d = nc.dram_tensor("x1_d", (N, D), F32, kind="Internal").ap()
        xf_d = nc.dram_tensor("xf_d", (N, D), F32, kind="Internal").ap()
        hs_d = nc.dram_tensor("hs_d", ((TILES + 1) * CAP, D), F32, kind="Internal").ap()
        ys_d = nc.dram_tensor("ys_d", ((TILES + 1) * CAP, D), F32, kind="Internal").ap()

        ident = sb("ident", [128, 128], F32)
        identb = sb("identb", [128, 128], BF16)
        cmask = sb("cmask", [P, 126], BF16)
        before = sb("before", [P, P], BF16)
        onesb = sb("onesb", [P, P], BF16)

        tri8 = sb("tri8", [P, E, E], F32)
        shift8 = sb("shift8", [P, E], F32)
        iota8 = sb("iota8", [P, E], F32)
        capk = sb("capk", [P, K_OVER], F32)
        lnT = sb("lnT", [128, 4 * DC], F32)
        rows = sb("rows", [4 * DC, 128], F32)
        b1T = sb("b1T", [128, E * DF // 128], F32)
        wg = sb("wg", [128, DC, E], F32)
        bc = [sb(f"bc{i}", [P, D], F32) for i in range(2)]
        onesr = sb("onesr", [P, 2], F32R)
        big = sb("big", [P, 2], BF16)
        bigi = sb("bigi", [1, 2], I32)
        stats = sb("stats", [P, C, 2, 6], F32)
        mvx = sb("mvx", [P, C, 2], F32)
        rx = sb("rx", [P, 2, C], F32)
        mv = sb("mv", [P, 2], F32)
        rstd = sb("rstd", [P, 1], F32)
        var = sb("var", [P, C], F32)
        root = sb("root", [P, C], F32)
        newt = sb("newt", [P, C], F32)
        dinv = sb("dinv", [P, C], F32)
        dtmp = sb("dtmp", [P, 2, C], F32)
        negmax = sb("negmax", [P, 2, 1], F32)
        smax = sb("smax", [P, 2, 1], F32)
        ssum = sb("ssum", [P, 2, 1], F32)
        rsum = sb("rsum", [P, 2, 1], F32)
        wtok = sb("wtok", [P, C], F32)
        eidx = sb("eidx", [P, C], I32)
        slot = sb("slot", [P, C], I32)
        slot1 = sb("slot1", [P, C], I32)
        over = sb("over", [1, 1 + K_OVER], I32)

        raw = [sb(f"raw{i}", [128, CH], F32) for i in range(F_RAWS)]
        whi = [sb(f"whi{i}", [128, CH], F32R) for i in range(F_SLOTS)]
        wlo = [sb(f"wlo{i}", [128, CH], F32R) for i in range(F_SLOTS)]

        RB = 7680
        R0 = region("r0", RB + 608,
                    [("S", [P, C, NP], I32), ("ohs", [P, EU, 626], BF16), ("ohd", [P, EU, HALF], BF16),
                     ("zero", [128, D], F32)],
                    [("agh", [128, DC, NP], F32R), ("agl", [128, DC, NP], F32R)],
                    [("hTh", [128, DC, NP], F32R), ("hTl", [128, DC, NP], F32R), ("aff0", [128, DC, P], F32)],
                    [("pr", [P, 3, NP - 2], F32), ("pTh", [P, C, NP], F32R), ("pTl", [P, C, NP], F32R)],
                    [("raw2", [128, CH], F32), ("raw3", [128, CH], F32),
                     ("hid", [128, 2, FW], F32), ("bia", [128, 2, JW, CAP], F32), ("ysb", [128, D], F32),
                     ("rt", [P, 10, 48], F32), ("tp", [P, E, E], F32)])
        R1 = region("r1", RB,
                    [("xnh", [P, C, D], F32R), ("xnl", [P, C, D], F32R)],
                    [("xf", [P, C, D], F32), ("n1", [P, C, D], F32)],
                    [("qh", [128, PAIRS, NP], F32R), ("ql", [128, PAIRS, NP], F32R)],
                    [("whi3", [128, CH], F32R), ("wlo3", [128, CH], F32R),
                     ("hs", [128, D], F32), ("hgf", [128, DC, CAP], F32),
                     ("hgh", [128, DC, CAP], F32R), ("hgl", [128, DC, CAP], F32R)])
        R2 = region("r2", RB,
                    [("cint", [P, C, HALF], I32), ("clo", [P, C, HALF], I32), ("chi", [P, C, HALF], I32),
                     ("ei", [P, 2, EC], I32), ("ef", [P, 4, EC], F32), ("iota16", [P, 626], F16)],
                    [("Sh", [P, C, NP], F32R), ("Sl", [P, C, NP], F32R), ("aff1", [128, DC, P], F32)],
                    [("whif", [128, CH], F32R), ("wlof", [128, CH], F32R)],
                    [("kh", [128, PAIRS, NP], F32R), ("kl", [128, PAIRS, NP], F32R)],
                    [("x2", [P, C, D], F32), ("base", [P, C, D], F32)])
        R3 = region("r3", RB,
                    [("xs", [P, C, D], F32), ("tmp", [P, 2, D], F32),
                     ("b1r", [96, 2, 128], F32)],
                    [("vh", [P, C, D], F32R), ("vl", [P, C, D], F32R)],
                    [("n2", [P, C, D], F32), ("h2T", [128, DC, NP], F32)],
                    [("hTTh", [128, DF // 128, CAP], F32R), ("hTTl", [128, DF // 128, CAP], F32R)])
        raw += [R0["raw2"], R0["raw3"]]
        front_w = [(whi[i], wlo[i]) for i in range(F_SLOTS)] + [(R2["whif"], R2["wlof"])]
        whi += [R1["whi3"]]
        wlo += [R1["wlo3"]]
        whi, wlo = ([t[(n + E_SLOT) % SLOTS] for n in range(SLOTS)] for t in (whi, wlo))
        S, ohs, ohd = R0["S"], R0["ohs"], R0["ohd"]
        ag = (R0["agh"], R0["agl"])
        hT = (R0["hTh"], R0["hTl"])
        pr, pT = R0["pr"], (R0["pTh"], R0["pTl"])
        hid, bia, ysb = R0["hid"], R0["bia"], R0["ysb"]
        xn = (R1["xnh"], R1["xnl"])
        xf, n1 = R1["xf"], R1["n1"]
        q = (R1["qh"], R1["ql"])
        hs, hgf, hg = R1["hs"], R1["hgf"], (R1["hgh"], R1["hgl"])
        cint, clo, chi, ei, ef = (R2[n] for n in ("cint", "clo", "chi", "ei", "ef"))
        iota16 = R2["iota16"]
        Sd = (R2["Sh"], R2["Sl"])
        k_ = (R2["kh"], R2["kl"])
        x2, base = R2["x2"], R2["base"]
        xs, tmp, b1r = R3["xs"], R3["tmp"], R3["b1r"]
        aff = (R0["aff0"], R2["aff1"])
        v = (R3["vh"], R3["vl"])
        n2, h2T = R3["n2"], R3["h2T"]
        rt, tp = R0["rt"], R0["tp"]
        hTT = (R3["hTTh"], R3["hTTl"])

        ps = ctx.enter_context(nc.psum_tensor("ps", [128, 8, 512], F32))

        def two(b, rows_=128):
            return ps[0:rows_, b:b + 2, 0:HALF]

        def wide(b, rows_):
            return ps[0:rows_, b:b + 2, 0:HB]

        def halves(t):
            return t.rearrange("p (a b) -> p a b", a=2)

        def blocks(b, rows_, n, width=128):
            flat = ps[0:rows_, b:b + 2, :].rearrange("p a b -> p (a b)")
            return flat[:, 0:n * 128].rearrange("p (n w) -> p n w", w=128)[:, :, 0:width]

        def turned_parts(u):
            c, nb = u % C, min(u % C + 1, 4)
            parts = [(blocks(4 + u % 2, P, nb, P), 0, nb)]
            if c == 4:
                parts.append((ps[0:P, 6:7, 384:384 + P], 4, 1))
            return parts

        def score_banks(u):
            h, c = divmod(u, C)
            return (c + 2 * (h % 2)) % 4

        def score_rows(u):
            b = score_banks(u)
            if u % C < 4:
                return ps[0:P, b, :]
            return ps[0:P, b:b + 2, :].rearrange("p a b -> p (a b)")

        UNITS = H * C

        s_edges, s_x, s_rows, s_b1r, s_wg, s_bc = (sem(n) for n in
                                                   ("edges_in", "x_in", "rows_in", "b1_in", "wg_in", "bias_in"))
        s_bp = sem("bp_in")
        s_zero, s_x1st, s_xfst, s_xfld, s_x1ld = (sem(n) for n in
                                                  ("hs_zeroed", "x1_stored", "xf_stored", "xf_back", "x1_back"))
        s_iota, s_const, s_pool = sem("columns_numbered"), sem("consts_made"), sem("pool_steps")
        s_raw = [sem(f"raw_in{i}") for i in range(RAWS)]
        s_fhi, s_flo0, s_flo = sem("front_hi"), sem("front_lo_first"), sem("front_lo")
        s_var, s_root = sem("variances_made"), sem("roots_made")
        s_vec, s_act = sem("vector_steps"), sem("scalar_steps")
        s_oh, s_ohused = sem("onehots_made"), sem("onehots_used")
        s_cint, s_cdec, s_cadd = sem("counts_read"), sem("counts_decoded"), sem("counts_added")
        s_ones, s_big, s_bigs, s_bigi = (sem(n) for n in ("ones_made", "big_marked", "big_summed", "big_known"))
        s_S, s_deg, s_dinv, s_Shi, s_Slo = (sem(n) for n in ("adj_made", "deg_done", "dinv_made", "adj_hi", "adj_lo"))
        s_ln0, s_xnh, s_xnl, s_xb = (sem(n) for n in ("x_normed", "xn_hi", "xn_lo", "x_plus_b2"))
        s_misc, s_miscev = sem("vectors_turned"), sem("vectors_read")
        s_agg, s_aggh, s_aggl = sem("aggregated"), sem("agg_hi", ), sem("agg_lo")
        s_tb, s_xw, s_t, s_hh, s_hl = sem("hidden_biased"), sem("transformed"), sem("hidden_scaled"), sem("hidden_hi"), sem("hidden_lo")
        s_x1, s_xf, s_n1, s_xfb = sem("x1_made"), sem("xf_made"), sem("n1_made"), sem("xf_plus_bp")
        s_n1T, s_aff, s_hTh, s_hTl, s_pad = (sem(n) for n in ("n1_turned", "h_scaled", "hT_hi", "hT_lo", "hT_padded"))
        s_pj, s_pjh, s_pjl = sem("projected"), sem("projected_hi"), sem("projected_lo")
        s_sc, s_rmx, s_mx, s_ex, s_rs, s_nm = (sem(n) for n in ("scores_done", "max_made", "max_scaled", "exp_made", "sum_inverted", "probs_normed"))
        s_tr, s_trh, s_trl, s_pv, s_pvh, s_pvl = (sem(n) for n in (
            "probs_turned", "probs_hi", "probs_lo", "heads_done", "heads_hi", "heads_lo"))
        s_ptz = sem("probs_padded")
        s_wp, s_x2, s_base, s_n2, s_n2T, s_h2T, s_gate = (sem(n) for n in (
            "attn_projected", "x2_made", "base_made", "n2_made", "n2_turned", "h2T_made", "gates_done"))
        s_slot, s_oh8, s_rank, s_route = sem("rows_chosen"), sem("choice_made"), sem("ranks_done"), sem("routed")
        s_scat, s_b2g, s_base2 = sem("tokens_sent"), sem("b2_in"), sem("base_with_b2")
        s_hs0, s_hs, s_hgT, s_hga, s_hgh, s_hgl = (sem(n) for n in (
            "first_tile_in", "tile_in", "tile_turned", "tile_scaled", "tile_hi", "tile_lo"))
        s_used, s_mhi, s_mlo = (sem(n) for n in ("chunks_used", "expert_hi", "expert_lo"))
        s_hidev, s_hidT, s_bia, s_hTh2, s_hTl2 = (sem(n) for n in (
            "hid_read", "hid_turned", "hid_biased", "hidT_hi", "hidT_lo"))
        s_yg = [sem(f"y_back{c}") for c in range(C)]
        s_yev, s_yst, s_ylast, s_zt, s_fin, s_out = (sem(n) for n in (
            "y_read", "y_stored", "last_y_stored", "zeros_made", "out_made", "out_stored"))

        tok = lambda a: a.rearrange("(c p) d -> p c d", p=P)
        mat = lambda a: a.rearrange("(c p) f -> p c f", p=128)
        head = lambda a: a.rearrange("h (c p) s -> c p h s", p=128)
        W1v = W1.rearrange("e (c p) f -> e p c f", p=128)
        W2v = W2.rearrange("e (j p) d -> e p j d", p=128)
        edge = lambda a: a.rearrange("(p c) -> p c", p=P)
        row = lambda a: a.rearrange("(a n) -> a n", a=1)
        rowc = lambda a: a.rearrange("(c p) -> c p", p=128)

        def wview(t):
            return t[:, :].rearrange("p (c f) -> p c f", c=3)

        class Count:
            def __init__(self, eng, s):
                self.eng, self.s, self.n = eng, s, 0

            def __call__(self, ins):
                self.n += 1
                ins.then_inc(self.s, 1)
                self.eng.wait_ge(self.s, self.n)

        def split(n):
            return (s_flo0, n) if n <= F_SLOTS else (s_flo, n - F_SLOTS)

        USED = {GNN1: (s_xw, C), GNN2: (s_xw, 2 * C), WV: (s_pj, C), WQ: (s_pj, C + PAIRS),
                WK: (s_pj, C + 2 * PAIRS), WP: (s_wp, C)}

        def slot_free(n):
            earlier = [m for m in range(n) if F_SLOT[m] == F_SLOT[n]]
            return USED[earlier[-1] // 2] if earlier else (s_agg, 2 * DC) if n >= F_SLOTS else None

        def raw_value(n):
            total = 0
            for m in range(n % F_RAWS, n + 1, F_RAWS):
                total += 48 if m // 2 in (WQ, WK, WV) else 16
            return total

        FULL = [raw_value(FRONT - 2), raw_value(FRONT - 1), 0, 0]

        block = ctx.enter_context(nc.Block())

        @block.sync
        def _(sp):
            sp.dma_start(ei[:, 0, :], edge(src)).then_inc(s_edges, 16)
            sp.dma_start(ei[:, 1, :], edge(dst)).then_inc(s_edges, 16)
            sp.dma_start(xs[:, :, :], tok(x)).then_inc(s_x, 16)
            for i, a in enumerate((ln1_g, ln1_b, ln2_g, ln2_b)):
                sp.dma_start(rows[i * DC:(i + 1) * DC, :], rowc(a)).then_inc(s_rows, 16)
            for i in range(2):
                sp.dma_start(b1r[:, i, :], b1.rearrange("e (j p) -> (e j) p", p=128)[96 * i:96 * i + 96, :]
                             ).then_inc(s_b1r, 16)
            sp.dma_start(wg[:, :, :], mat(Wg)).then_inc(s_wg, 16)

            mats = (gW1, gW2, Wv, Wq, Wk, Wp)
            for n in range(FRONT):
                m, half = divmod(n, 2)
                r = raw[n % F_RAWS]
                if n >= F_RAWS:
                    sp.wait_ge(*split(n - F_RAWS + 1))
                if m in (WQ, WK, WV):
                    for c in range(3):
                        sp.dma_start(wview(r)[:, c, :].rearrange("p (h s) -> p h s", h=H),
                                     head(mats[m])[3 * half + c]).then_inc(s_raw[n % F_RAWS], 16)
                else:
                    sp.dma_start(wview(r), mat(mats[m])[:, 3 * half:3 * half + 3, :]
                                 ).then_inc(s_raw[n % F_RAWS], 16)

            def weights(e, t):
                for n in range(SCH):
                    if not isinstance(t, int) or n >= RAWS:
                        sp.wait_ge(s_mlo, SCH * t + n + 1 - RAWS)
                    elif n < F_RAWS:
                        sp.wait_ge(*split(FRONT - F_RAWS + n + 1))
                    else:
                        sp.wait_ge(s_pv, 2 * H)
                    r = raw[n % RAWS]
                    if n < FCH:
                        sp.dma_start(r[:, :].rearrange("p (c f) -> p c f", c=DC),
                                     W1v[e, :, :, n * FW:(n + 1) * FW]).then_inc(s_raw[n % RAWS], 16)
                    else:
                        sp.dma_start(wview(r), W2v[e, :, JW * (n - FCH):JW * (n - FCH + 1), :]
                                     ).then_inc(s_raw[n % RAWS], 16)

            weights(0, 0)
            with sp.Fori(1, E) as t:
                weights(t, t)
            sp.wait_ge(s_route, 1)
            n_over = sp.value_load(over[0:1, 0:1], min_val=0, max_val=K_OVER)
            with sp.Fori(0, K_OVER) as s:
                e = sp.value_load(over[0:1, bass.ds(s + 1, 1)], min_val=0, max_val=E - 1)
                with sp.If(s < n_over):
                    weights(e, s + E)
            for c in range(C):
                sp.wait_ge(s_fin, c + 1)
                sp.dma_start(tok(out)[:, c, :], x2[:, c, :]).then_inc(s_out, 16)
            sp.wait_ge(s_out, 16 * C)

        @block.gpsimd
        def _(g):
            step = Count(g, s_pool)
            gp = nc.gpsimd
            gp.iota(iota16[:, :], pattern=[[1, 626]], base=0, channel_multiplier=0,
                    allow_small_or_imprecise_dtypes=True).then_inc(s_iota, 1)
            step(gp.memset(ident[:, :], 0.0))
            gp.affine_select(out=ident[:, :], in_=ident[:, :], compare_op=ALU.not_equal, fill=1.0,
                             base=0, pattern=[[-1, 128]], channel_multiplier=1).then_inc(s_const, 1)
            step(gp.memset(identb[:, :], 0.0))
            gp.affine_select(out=identb[:, :], in_=identb[:, :], compare_op=ALU.not_equal, fill=1.0,
                             base=0, pattern=[[-1, 128]], channel_multiplier=1).then_inc(s_const, 1)
            for i, a in enumerate((gb1, gb2)):
                g.dma_start(bc[i][:, :], row(a).broadcast_to((P, D))).then_inc(s_bc, 16)
            gp.memset(onesb[:, :], 1.0).then_inc(s_const, 1)
            step(gp.memset(cmask[:, :], 0.0))
            gp.affine_select(out=cmask[:, :], in_=cmask[:, :], compare_op=ALU.is_ge, fill=-1e30,
                             base=0, pattern=[[-1, 126]], channel_multiplier=1).then_inc(s_const, 1)
            step(gp.memset(before[:, :], 1.0))
            gp.affine_select(out=before[:, :], in_=before[:, :], compare_op=ALU.is_gt, fill=0.0,
                             base=0, pattern=[[1, P]], channel_multiplier=-1).then_inc(s_const, 1)
            gp.iota(shift8[:, :], pattern=[[-CAP, E]], base=CAP * (E - 1), channel_multiplier=0,
                    allow_small_or_imprecise_dtypes=True).then_inc(s_const, 1)
            step(gp.memset(tri8[:, :, :], float(CAP)))
            gp.affine_select(out=tri8[:, :, :], in_=tri8[:, :, :], compare_op=ALU.is_gt, fill=0.0,
                             base=0, pattern=[[1, E], [-1, E]], channel_multiplier=0).then_inc(s_const, 1)
            gp.iota(iota8[:, :], pattern=[[1, E]], base=0, channel_multiplier=0,
                    allow_small_or_imprecise_dtypes=True).then_inc(s_const, 1)
            gp.iota(capk[:, :], pattern=[[CAP, K_OVER]], base=CAP, channel_multiplier=0,
                    allow_small_or_imprecise_dtypes=True).then_inc(s_const, 1)

            step(gp.memset(S[:, :, :], 0))
            def add_counts(gr):
                g.wait_ge(s_cdec, gr + 1)
                gp.tensor_tensor(S[:, :, 0:HALF], S[:, :, 0:HALF], clo[:, :, :], ALU.add)
                gp.tensor_tensor(S[:, :, HALF:NP], S[:, :, HALF:NP], chi[:, :, :], ALU.add).then_inc(s_cadd, 1)

            for n in range(F_SLOTS):
                if n < len(GROUPS) - 1:
                    add_counts(n)
                g.wait_ge(s_fhi, n + 1)
                w_hi, w_lo = front_w[F_SLOT[n]]
                gp.tensor_tensor(w_lo[:, :], raw[n % F_RAWS][:, :], w_hi[:, :], ALU.subtract).then_inc(s_flo0, 1)

            g.wait_ge(s_bc, 32)
            g.wait_ge(s_ln0, C)
            for c in range(C):
                gp.tensor_tensor(xs[:, c, :], xs[:, c, :], bc[1][:, :], ALU.add).then_inc(s_xb, 1)
            g.wait_ge(s_xb, C)
            g.dma_start(bc[1][:, :], row(bp).broadcast_to((P, D))).then_inc(s_bp, 16)

            g.wait_ge(s_bp, 16)
            for c in range(C):
                g.wait_ge(s_n1, c + 1)
                gp.tensor_tensor(xf[:, c, :], xf[:, c, :], bc[1][:, :], ALU.add).then_inc(s_xfb, 1)
                if c == 2:
                    g.wait_ge(s_x1, C)
                    g.dma_start(tok(x1_d), xs[:, :, :]).then_inc(s_x1st, 16)
            g.wait_ge(s_xfb, C)
            g.dma_start(tok(xf_d), xf[:, :, :]).then_inc(s_xfst, 16)

            g.wait_ge(s_sc, UNITS)
            g.wait_ge(s_xfst, 16)
            g.wait_ge(s_x1st, 16)
            g.dma_start(x2[:, :, :], tok(xf_d)).then_inc(s_xfld, 16)
            g.dma_start(base[:, :, :], tok(x1_d)).then_inc(s_x1ld, 16)
            g.wait_ge(s_x1ld, 16)
            for c in range(C):
                g.wait_ge(s_x2, c + 1)
                gp.tensor_tensor(base[:, c, :], base[:, c, :], x2[:, c, :], ALU.add).then_inc(s_base, 1)

            g.wait_ge(s_zero, 16 * (TILES + 1 + K_OVER))
            g.wait_ge(s_slot, 1)
            g.wait_ge(s_n2, C)
            for c in range(C):
                g.indirect_dma_start(out=hs_d[:, :], out_offset=bass.IndirectOffsetOnAxis(ap=slot[:, c:c + 1], axis=0),
                                     in_=n2[:, c, :], in_offset=None).then_inc(s_scat, 16)

            g.wait_ge(s_base, C)
            for c in range(C):
                g.indirect_dma_start(out=x2[:, c, :], out_offset=None, in_=b2[:, :],
                                     in_offset=bass.IndirectOffsetOnAxis(ap=eidx[:, c:c + 1], axis=0)
                                     ).then_inc(s_b2g, 16)

            def tile(t):
                g.wait_ge(s_hgT, t + 1)
                g.dma_start(hs[0:CAP, :], hs_d[bass.ds((t + 1) * CAP, CAP), :]).then_inc(s_hs, 16)
                g.wait_ge(s_yev, 2 * t + 2)
                g.dma_start(ys_d[bass.ds(t * CAP, CAP), :], ysb[0:CAP, :]).then_inc(s_yst, 16)

            g.wait_ge(s_route, 1)
            n_over = g.value_load(over[0:1, 0:1], min_val=0, max_val=K_OVER)
            with g.Fori(0, E) as t:
                tile(t)
            with g.Fori(0, K_OVER) as s:
                with g.If(s < n_over):
                    tile(s + E)
            g.wait_ge(s_yev, 2 * (n_over + E) + 2)
            g.dma_start(ys_d[bass.ds((n_over + E) * CAP, CAP), :], ysb[0:CAP, :]).then_inc(s_ylast, 16)
            g.wait_ge(s_ylast, 16)
            g.wait_ge(s_base2, C)
            for c in range(C):
                g.indirect_dma_start(out=x2[:, c, :], out_offset=None, in_=ys_d[:, :],
                                     in_offset=bass.IndirectOffsetOnAxis(ap=slot1[:, c:c + 1], axis=0)
                                     ).then_inc(s_yg[c], 16)
            for c in range(C):
                g.wait_ge(s_yg[c], 16)

        @block.scalar
        def _(a):
            act = nc.scalar

            def hi(out_, in_, s, func=ACT.Copy):
                act.activation(out_, in_, func).then_inc(s, 1)

            roots = [0]

            def root_of(n=1):
                roots[0] += 1
                a.wait_ge(s_var, roots[0])
                act.activation(root[:, 0:n], var[:, 0:n], ACT.Sqrt).then_inc(s_root, 1)

            def front(n):
                if n >= F_SLOTS:
                    a.wait_ge(*slot_free(n))
                a.wait_ge(s_raw[n % F_RAWS], raw_value(n))
                hi(front_w[F_SLOT[n]][0][:, :], raw[n % F_RAWS][:, :], s_fhi)

            a.wait_ge(s_zt, 1)
            for t in range(TILES + 1):
                a.dma_start(hs_d[t * CAP:(t + 1) * CAP, :], R0["zero"][0:CAP, :]).then_inc(s_zero, 16)
            for t in range(E + 1, TILES + 1):
                a.dma_start(ys_d[t * CAP:(t + 1) * CAP, :], R0["zero"][0:CAP, :]).then_inc(s_zero, 16)

            for g in range(len(GROUPS)):
                a.wait_ge(s_ohused, EU * sum(GROUPS[:g + 1]))
                if g:
                    a.wait_ge(s_cdec, g)
                act.activation(cint[:, :, :], ps[0:P, 0:C, 0:HALF], ACT.Copy).then_inc(s_cint, 1)
                if g == 0:
                    front(0)
                    a.wait_ge(s_misc, 1)
                    act.activation(lnT[:, :], ps[:, 6, 0:4 * DC], ACT.Copy).then_inc(s_miscev, 1)
                    act.activation(b1T[:, :], ps[:, 6, 128:320], ACT.Copy).then_inc(s_miscev, 1)
                if g == 1:
                    front(1)
            for c in range(C):
                a.wait_ge(s_S, C)
                act.activation(Sd[0][:, c, :], S[:, c, :], ACT.Copy).then_inc(s_Shi, 1)
            root_of(C)
            root_of(C)
            for c in range(C):
                a.wait_ge(s_ln0, c + 1)
                hi(xn[0][:, c, :], tmp[:, c % 2, :], s_xnh)
            front(2)

            def agg(r):
                for m in range(DC):
                    a.wait_ge(s_agg, r * DC + m + 1)
                    if not r and not m:
                        a.wait_ge(s_Slo, C)
                        a.wait_ge(s_zero, 16 * (TILES + 1 + K_OVER))
                    hi(halves(ag[0][:, m, :]), two(2 * (m % 2)), s_aggh)

            agg(0)
            for c in range(C):
                a.wait_ge(s_t, c + 1)
                hi(xn[0][:, c, :], tmp[:, c % 2, :], s_hh)
            front(3)
            front(4)
            agg(1)

            def h_turned(c):
                a.wait_ge(s_n1T, c + 1)
                if c >= 2:
                    a.wait_ge(s_hTl, c - 1)
                for m in range(DC):
                    act.activation(aff[c % 2][:, m, :], blocks(2 * (c % 2), 128, DC, P)[:, m, :], ACT.Identity,
                                   scale=lnT[:, m:m + 1], bias=lnT[:, DC + m:DC + m + 1]).then_inc(s_aff, 1)
                a.wait_ge(s_aff, DC * (c + 1))
                hi(hT[0][:, :, c * P:(c + 1) * P], aff[c % 2][:, :, :], s_hTh)

            def v_out(c):
                a.wait_ge(s_pj, c + 1)
                if not c:
                    a.wait_ge(s_x1st, 16)
                hi(v[0][:, c, :].rearrange("p (a b) -> p a b", a=2), wide(4 + 2 * (c % 2), P), s_pjh)

            for i in range(C + 1):
                if i == 4:
                    front(5)
                root_of(2)
                if i >= 2:
                    h_turned(i - 2)
            v_out(0)
            h_turned(4)
            v_out(1)
            front(6)
            v_out(2)
            front(7)
            v_out(3)
            v_out(4)

            def pair_out(r, m):
                a.wait_ge(s_pj, C + r * PAIRS + m + 1)
                if not r and not m:
                    a.wait_ge(s_xfst, 16)
                hi(halves((q, k_)[r][0][:, m, :]), two(2 * (m % 2)), s_pjh)

            for r in range(2):
                for m in range(PAIRS):
                    pair_out(r, m)
                    if (r, m) in PAIR_FRONT:
                        front(PAIR_FRONT[r, m])
            front(11)

            def split_hi(n, t):
                if isinstance(t, int) and n < SLOTS:
                    a.wait_ge(*USED[WK if n == 0 else WP])
                else:
                    a.wait_ge(s_used, SCH * t + n + 1 - SLOTS)
                a.wait_ge(s_raw[n % RAWS], (SCH // RAWS * 16) * t + FULL[n % RAWS] + 16 * (n // RAWS + 1))
                hi(whi[n % SLOTS][:, :], raw[n % RAWS][:, :], s_mhi)

            def turned(u):
                h, c = divmod(u, C)
                a.wait_ge(s_tr, u + 1)
                if u == 0:
                    a.wait_ge(s_ptz, 1)
                elif c == 0 and h or c == 2 and h:
                    a.wait_ge(s_pv, 2 * h - 1 + c // 2)
                for place, b0, nb in turned_parts(u):
                    ins = act.activation(pT[0][:, b0:b0 + nb, c * P:(c + 1) * P], place, ACT.Copy)
                ins.then_inc(s_trh, 1)

            def head_out(h):
                r0 = 64 * (h % 2)
                a.wait_ge(s_pv, 2 * h + 2)
                hi(halves(q[0][r0:r0 + 64, h // 2, :]), ps[r0:r0 + 64, 6:8, 0:HALF], s_pvh)

            for i in range(UNITS + 5):
                if 3 <= i < UNITS + 3:
                    turned(i - 3)
                if i < UNITS:
                    c = i % C
                    n = (c + 1) * P + (c + 1) % 2
                    a.wait_ge(s_mx, i + 1)
                    if i >= 3:
                        a.wait_ge(s_tr, i - 2)
                    act.activation(pr[:, i % 3, 0:n], score_rows(i)[:, 0:n], ACT.Exp, bias=negmax[:, i % 2, :],
                                   scale=float(D) ** -0.5, accum_out=ssum[:, i % 2, :]).then_inc(s_ex, 1)
                if i >= 9 and (i - 9) % C == 0:
                    head_out((i - 9) // C)

            split_hi(0, 0)

            def h2_turned(c):
                a.wait_ge(s_n2T, c + 1)
                for m in range(DC):
                    act.activation(h2T[:, m, c * P:(c + 1) * P], blocks(0, 128, DC, P)[:, m, :], ACT.Identity,
                                   scale=lnT[:, 2 * DC + m:2 * DC + m + 1],
                                   bias=lnT[:, 3 * DC + m:3 * DC + m + 1]).then_inc(s_h2T, 1)

            for c in range(C):
                if c == C - 1:
                    split_hi(1, 0)
                root_of()
                if c >= 1:
                    h2_turned(c - 1)
            h2_turned(C - 1)
            split_hi(2, 0)
            a.wait_ge(s_oh8, 1)
            act.activation(rt[:, 7, 0:C], rt[:, 6, 0:C], ACT.Exp).then_inc(s_act, 1)

            def tile_in(n_in, n_a):
                a.wait_ge(s_hgT, n_in)
                for m in range(DC):
                    act.activation(hgf[:, m, :], blocks(6, 128, DC, CAP)[:, m, :], ACT.Identity,
                                   scale=lnT[:, 2 * DC + m:2 * DC + m + 1],
                                   bias=lnT[:, 3 * DC + m:3 * DC + m + 1]).then_inc(s_hga, 1)
                a.wait_ge(s_hga, n_a)
                hi(hg[0][:, :, :], hgf[:, :, :], s_hgh)

            a.wait_ge(s_scat, 16 * C)
            a.dma_start(hs[0:CAP, :], hs_d[0:CAP, :]).then_inc(s_hs0, 16)
            split_hi(3, 0)
            tile_in(1, DC)

            def tile(t, first):
                for k in range(SCH):
                    if k == 0:
                        for n in range(AHEAD if first else 0, AHEAD):
                            split_hi(n, t)
                        if not first:
                            a.wait_ge(s_used, SCH * t)
                            a.wait_ge(s_yst, 16 * t)
                        act.activation(ysb[0:CAP, 0:HB], ps[0:CAP, 4, 0:HB], ACT.Copy).then_inc(s_yev, 1)
                    if k + AHEAD < SCH and not (first and k == 0):
                        split_hi(k + AHEAD, t)
                    if 1 <= k <= FCH:
                        a.wait_ge(s_used, SCH * t + k)
                        if k >= 3:
                            a.wait_ge(s_hidT, FCH * t + k - 2)
                        act.activation(hid[0:CAP, (k - 1) % 2, :], ps[0:CAP, (k - 1) % 2, 0:FW], ACT.Copy
                                       ).then_inc(s_hidev, 1)
                    if 2 <= k <= FCH + 1:
                        a.wait_ge(s_bia, FCH * t + k - 1)
                        hi(hTT[0][:, JW * (k - 2):JW * (k - 1), :], bia[:, k % 2, :, :], s_hTh2, ACT.Relu)
                    if k == FCH + 2:
                        tile_in(t + 2, DC * t + 2 * DC)

            tile(0, True)
            with a.Fori(1, E) as t:
                tile(t, False)
            a.wait_ge(s_route, 1)
            n_over = a.value_load(over[0:1, 0:1], min_val=0, max_val=K_OVER)
            with a.Fori(0, K_OVER) as s:
                with a.If(s < n_over):
                    tile(s + E, False)
            a.wait_ge(s_used, SCH * (n_over + E))
            a.wait_ge(s_yst, 16 * (n_over + E))
            act.activation(ysb[0:CAP, 0:HB], ps[0:CAP, 4, 0:HB], ACT.Copy).then_inc(s_yev, 1)

        @block.vector
        def _(d):
            dve = nc.vector
            step = Count(d, s_vec)

            def lo(out_, in_, hi_, s, relu=False):
                if relu:
                    dve.scalar_tensor_tensor(out_, in_, 0.0, hi_, ALU.max, ALU.subtract).then_inc(s, 1)
                else:
                    dve.tensor_tensor(out_, in_, hi_, ALU.subtract).then_inc(s, 1)

            def front(n):
                d.wait_ge(s_fhi, n + 1)
                w_hi, w_lo = front_w[F_SLOT[n]]
                lo(w_lo[:, :], raw[n % F_RAWS][:, :], w_hi[:, :], s_flo)

            def rsqrt(in_, by, op, out_, n):
                rsqrts[0] += 1
                dve.tensor_scalar(var[:, 0:n], in_, by, None, op).then_inc(s_var, 1)
                d.wait_ge(s_root, rsqrts[0])
                step(dve.reciprocal(root[:, 0:n], root[:, 0:n]))
                step(dve.scalar_tensor_tensor(newt[:, 0:n], root[:, 0:n], -0.5, root[:, 0:n], ALU.mult, ALU.mult))
                step(dve.tensor_tensor(newt[:, 0:n], newt[:, 0:n], var[:, 0:n], ALU.mult))
                step(dve.scalar_tensor_tensor(out_, newt[:, 0:n], 1.5, root[:, 0:n], ALU.add, ALU.mult))

            rsqrts = [0]

            def norm(out_, in_):
                dve.bn_stats(stats[:, 0, 0, :], in_[:, 0:HB])
                step(dve.bn_stats(stats[:, 0, 1, :], in_[:, HB:D]))
                step(dve.bn_aggr(mv[:, :], stats[:, 0, :, :]))
                rsqrt(mv[:, 1:2], EPS, ALU.add, rstd[:, :], 1)
                return dve.tensor_scalar(out_, in_, mv[:, 0:1], rstd[:, :], ALU.subtract, ALU.mult)

            dve.memset(R0["zero"][:, :], 0.0).then_inc(s_zt, 1)
            step(dve.memset(ps[:, 4:6, 0:HB], 0.0))
            d.wait_ge(s_edges, 32)
            step(dve.tensor_copy(ef[:, 0:2, :], ei[:, :, :]))
            step(dve.tensor_scalar(ef[:, 2, :], ef[:, 1, :], float(HALF), None, ALU.is_ge))
            step(dve.scalar_tensor_tensor(ef[:, 3, :], ef[:, 2, :], -float(HALF), ef[:, 1, :], ALU.mult, ALU.add))
            step(dve.tensor_scalar(ef[:, 2, :], ef[:, 2, :], float(RADIX - 1), 1.0, ALU.mult, ALU.add))

            def onehots(i, first):
                for j in range(EU):
                    at = bass.ds(i * EU + j, 1)
                    if not first:
                        d.wait_ge(s_ohused, EU * i + j - (EU - 1))
                    dve.tensor_scalar(ohs[:, j, :], iota16[:, :], ef[:, 0, at], None, ALU.is_equal)
                    dve.tensor_scalar(ohd[:, j, :], iota16[:, 0:HALF], ef[:, 3, at], ef[:, 2, at],
                                      ALU.is_equal, ALU.mult).then_inc(s_oh, 1)

            def decode(g):
                d.wait_ge(s_cint, g + 1)
                if g:
                    d.wait_ge(s_cadd, g)
                dve.tensor_scalar(clo[:, :, :], cint[:, :, :], RADIX - 1, None, ALU.bitwise_and)
                dve.tensor_scalar(chi[:, :, :], cint[:, :, :], 12, None, ALU.logical_shift_right).then_inc(s_cdec, 1)

            d.wait_ge(s_iota, 1)
            at = 0
            for g, steps in enumerate(GROUPS):
                onehots(at, g == 0)
                if g:
                    decode(g - 1)
                with d.Fori(at + 1, at + steps) as i:
                    onehots(i, False)
                at += steps
            d.wait_ge(s_const, 9)
            dve.tensor_copy(onesr[:, :], onesb[:, 0:2]).then_inc(s_ones, 1)
            decode(len(GROUPS) - 1)
            d.wait_ge(s_cdec, len(GROUPS))
            dve.tensor_tensor(S[:, :, 0:HALF], S[:, :, 0:HALF], clo[:, :, :], ALU.add)
            step(dve.tensor_tensor(S[:, :, HALF:NP], S[:, :, HALF:NP], chi[:, :, :], ALU.add))
            for c in range(C):
                dve.tensor_tensor(S[:, c, c * P:(c + 1) * P], S[:, c, c * P:(c + 1) * P],
                                  ident[0:P, 0:P], ALU.add).then_inc(s_S, 1)
            for c in range(C):
                d.wait_ge(s_Shi, c + 1)
                lo(Sd[1][:, c, :], S[:, c, :], Sd[0][:, c, :], s_Slo)
            d.wait_ge(s_x, 16)
            for c in range(C):
                for i in range(2):
                    ins = dve.bn_stats(stats[:, c, i, :], xs[:, c, i * HB:(i + 1) * HB])
            step(ins)
            for c in range(C):
                ins = dve.bn_aggr(mvx[:, c, :], stats[:, c, :, :])
            step(ins)
            rsqrt(mvx[:, :, 1], EPS, ALU.add, rx[:, 0, :], C)
            d.wait_ge(s_deg, 1)
            deg = ps[0:P, 5, 0:2 * C].rearrange("p (c o) -> p c o", o=2)[:, :, 0]
            dve.tensor_scalar(dtmp[:, 0, :], deg, 0.0, None, ALU.is_gt)
            rsqrt(deg, 1.0, ALU.max, dtmp[:, 1, :], C)
            step(dve.tensor_tensor(dinv[:, :], dtmp[:, 0, :], dtmp[:, 1, :], ALU.mult))
            dve.tensor_tensor(rx[:, 1, :], rx[:, 0, :], dinv[:, :], ALU.mult).then_inc(s_dinv, 1)
            step(dve.reduce_max(mv[:, 0:1], deg, AX))
            dve.tensor_scalar(big[:, 0:1], mv[:, 0:1], float(BIG), None, ALU.is_ge).then_inc(s_big, 1)
            d.wait_ge(s_dinv, 1)

            for c in range(C + 1):
                if 2 <= c < C:
                    d.wait_ge(s_xnl, c - 1)
                if c < C:
                    dve.tensor_scalar(tmp[:, c % 2, :], xs[:, c, :], mvx[:, c, 0:1], rx[:, 1, c:c + 1],
                                      ALU.subtract, ALU.mult).then_inc(s_ln0, 1)
                if c:
                    d.wait_ge(s_xnh, c)
                    lo(xn[1][:, c - 1, :], tmp[:, (c - 1) % 2, :], xn[0][:, c - 1, :], s_xnl)
                if c == 1:
                    d.wait_ge(s_bigs, 1)
                    dve.tensor_copy(bigi[0:1, 0:1], ps[0:1, 4, 0:1]).then_inc(s_bigi, 1)

            def agg(r):
                for m in range(DC):
                    d.wait_ge(s_aggh, r * DC + m + 1)
                    lo(halves(ag[1][:, m, :]), two(2 * (m % 2)), halves(ag[0][:, m, :]), s_aggl)

            agg(0)
            d.wait_ge(s_bc, 32)
            for c in range(C):
                d.wait_ge(s_xw, c + 1)
                if c >= 2:
                    d.wait_ge(s_hl, c - 1)
                dve.scalar_tensor_tensor(tmp[:, c % 2, :].rearrange("p (a b) -> p a b", a=2), wide(4 + 2 * (c % 2), P),
                                         dinv[:, c:c + 1], bc[0][:, :].rearrange("p (a b) -> p a b", a=2),
                                         ALU.mult, ALU.add).then_inc(s_tb, 1)
                d.wait_ge(s_tb, c + 1)
                dve.tensor_scalar(tmp[:, c % 2, :], tmp[:, c % 2, :], 0.0, dinv[:, c:c + 1], ALU.max, ALU.mult
                                  ).then_inc(s_t, 1)
                d.wait_ge(s_hh, c + 1)
                lo(xn[1][:, c, :], tmp[:, c % 2, :], xn[0][:, c, :], s_hl)
            front(3)
            front(4)
            agg(1)
            d.wait_ge(s_xb, C)
            def h_turned(c):
                rows_ = slice(c * P, (c + 1) * P)
                d.wait_ge(s_hTh, c + 1)
                lo(hT[1][:, :, rows_], aff[c % 2][:, :, :], hT[0][:, :, rows_], s_hTl)

            def v_out(c):
                d.wait_ge(s_pjh, c + 1)
                lo(v[1][:, c, :].rearrange("p (a b) -> p a b", a=2), wide(4 + 2 * (c % 2), P),
                   v[0][:, c, :].rearrange("p (a b) -> p a b", a=2), s_pjl)

            for i in range(C + 1):
                if i < C:
                    d.wait_ge(s_xw, C + i + 1)
                    dve.scalar_tensor_tensor(xs[:, i, :].rearrange("p (a b) -> p a b", a=2), wide(4 + 2 * (i % 2), P),
                                             dinv[:, i:i + 1], xs[:, i, :].rearrange("p (a b) -> p a b", a=2),
                                             ALU.mult, ALU.add).then_inc(s_x1, 1)
                norms = [(1, xf[:, i - 1, :], n1[:, i - 1, :], s_n1)] if i else []
                norms += [(0, xs[:, i, :], xf[:, i, :], s_xf)] if i < C else []
                for k, in_, _, _ in norms:
                    if k == 0:
                        d.wait_ge(s_x1, i + 1)
                    elif i:
                        d.wait_ge(s_xf, i)
                    for half in range(2):
                        ins = dve.bn_stats(stats[:, k, half, :], in_[:, half * HB:(half + 1) * HB])
                step(ins)
                if i == 4:
                    front(5)
                for k, _, _, _ in norms:
                    ins = dve.bn_aggr(mvx[:, k, :], stats[:, k, :, :])
                step(ins)
                k0, k1 = min(n[0] for n in norms), max(n[0] for n in norms) + 1
                rsqrt(mvx[:, k0:k1, 1], EPS, ALU.add, rx[:, 0, k0:k1], k1 - k0)
                for k, in_, out_, s_ in norms:
                    dve.tensor_scalar(out_, in_, mvx[:, k, 0:1], rx[:, 0, k:k + 1], ALU.subtract, ALU.mult
                                      ).then_inc(s_, 1)
                if i >= 3:
                    h_turned(i - 3)
            h_turned(3)
            v_out(0)
            h_turned(4)
            for i in range(2):
                dve.memset(hT[i][:, :, N:NP].bitcast(F32), 0.0).then_inc(s_pad, 1)
            v_out(1)
            front(6)
            v_out(2)
            front(7)
            v_out(3)
            v_out(4)

            def pair_out(r, m):
                d.wait_ge(s_pjh, C + r * PAIRS + m + 1)
                lo(halves((q, k_)[r][1][:, m, :]), two(2 * (m % 2)), halves((q, k_)[r][0][:, m, :]), s_pjl)

            for r in range(2):
                for m in range(PAIRS):
                    pair_out(r, m)
                    if (r, m) in PAIR_FRONT:
                        front(PAIR_FRONT[r, m])
            front(11)
            d.wait_ge(s_pj, 2 * PAIRS + C)
            for i in range(2):
                for b in range(1, C, 2):
                    dve.memset(pT[i][:, b, b * P - 1:b * P].bitcast(F32), 0.0)
                last = dve.memset(pT[i][:, :, N:NP].bitcast(F32), 0.0)
            last.then_inc(s_ptz, 1)

            def turned(u):
                c = u % C
                d.wait_ge(s_trh, u + 1)
                cols = slice(c * P, (c + 1) * P)
                for place, b0, nb in turned_parts(u):
                    ins = dve.tensor_tensor(pT[1][:, b0:b0 + nb, cols], place,
                                            pT[0][:, b0:b0 + nb, cols], ALU.subtract)
                ins.then_inc(s_trl, 1)

            def head_out(h):
                r0 = 64 * (h % 2)
                d.wait_ge(s_pvh, h + 1)
                lo(halves(q[1][r0:r0 + 64, h // 2, :]), ps[r0:r0 + 64, 6:8, 0:HALF],
                   halves(q[0][r0:r0 + 64, h // 2, :]), s_pvl)

            for i in range(UNITS + 6):
                if i < UNITS:
                    c = i % C
                    n = (c + 1) * P + (c + 1) % 2
                    d.wait_ge(s_sc, i + 1)
                    dve.reduce_max(smax[:, i % 2, :], score_rows(i)[:, 0:n], AX).then_inc(s_rmx, 1)
                if i >= 10 and i % C == 0:
                    head_out(i // C - 2)
                if 1 <= i <= UNITS:
                    d.wait_ge(s_ex, i)
                    dve.reciprocal(rsum[:, i % 2, :], ssum[:, (i - 1) % 2, :]).then_inc(s_rs, 1)
                if i < UNITS:
                    d.wait_ge(s_rmx, i + 1)
                    dve.tensor_scalar(negmax[:, i % 2, :], smax[:, i % 2, :], -(float(D) ** -0.5), None,
                                      ALU.mult).then_inc(s_mx, 1)
                if 3 <= i < UNITS + 3:
                    turned(i - 3)
                if 1 <= i <= UNITS:
                    d.wait_ge(s_rs, i)
                    n = ((i - 1) % C + 1) * P
                    dve.tensor_scalar(pr[:, (i - 1) % 3, 0:n], pr[:, (i - 1) % 3, 0:n], rsum[:, i % 2, :], None,
                                      ALU.mult).then_inc(s_nm, 1)
            d.wait_ge(s_pv, 2 * H)

            def split_lo(n, t):
                d.wait_ge(s_mhi, SCH * t + n + 1)
                lo(wlo[n % SLOTS][:, :], raw[n % RAWS][:, :], whi[n % SLOTS][:, :], s_mlo)

            d.wait_ge(s_xfld, 16)
            split_lo(0, 0)
            for c in range(C):
                d.wait_ge(s_wp, c + 1)
                dve.tensor_tensor(x2[:, c, :].rearrange("p (a b) -> p a b", a=2), wide(4 + 2 * (c % 2), P),
                                  x2[:, c, :].rearrange("p (a b) -> p a b", a=2), ALU.add).then_inc(s_x2, 1)
                d.wait_ge(s_x2, c + 1)
                norm(n2[:, c, :], x2[:, c, :]).then_inc(s_n2, 1)
            split_lo(1, 0)

            d.wait_ge(s_gate, 1)
            lg = rt[:, 0, 0:C * E].rearrange("p (c e) -> p c e", e=E)
            mx8 = rt[:, 1, 0:C * E].rearrange("p (c e) -> p c e", e=E)
            ix8 = rt[:, 2, 0:C * E].rearrange("p (c e) -> p c e", e=E).bitcast(U32)
            ohe = rt[:, 3, 0:C * E].rearrange("p (c e) -> p c e", e=E)
            ef5 = rt[:, 6, 8:8 + C]
            step(dve.tensor_copy(lg, ps[0:P, 2, 0:C * E].rearrange("p (c e) -> p c e", e=E)))
            for c in range(C):
                last = dve.max(mx8[:, c, :], lg[:, c, :])
            step(last)
            for c in range(C):
                last = dve.max_index(ix8[:, c, :], mx8[:, c, :], lg[:, c, :])
            step(last)
            dve.tensor_tensor(rt[:, 6, 0:C], mx8[:, :, 0], mx8[:, :, 0], ALU.subtract)
            dve.tensor_copy(eidx[:, :], ix8[:, :, 0])
            step(dve.tensor_copy(ef5, ix8[:, :, 0]))
            ohb = rt[:, 4, 0:C * E // 2].bitcast(BF16).rearrange("p (c e) -> p c e", e=E)
            for to in (ohb, ohe):
                last = dve.tensor_tensor(to, iota8[:, :].rearrange("p (o e) -> p o e", o=1).broadcast_to((P, C, E)),
                                         ef5.rearrange("p (c o) -> p c o", o=1).broadcast_to((P, C, E)), ALU.is_equal)
                last.then_inc(s_oh8, 1)
            d.wait_ge(s_oh8, 2)
            d.wait_ge(s_act, 1)
            step(dve.reciprocal(rt[:, 7, 8:8 + C], rt[:, 7, 0:C]))
            dve.tensor_tensor(wtok[:, :], rt[:, 7, 0:C], rt[:, 7, 8:8 + C], ALU.mult)
            split_lo(2, 0)
            d.wait_ge(s_rank, 1)
            rank8 = ps[0:P, 3, 0:C * E].rearrange("p (c e) -> p c e", e=E)
            cnt = ps[0:P, 3, C * E:C * E + E]
            nov = rt[:, 5, 0:E]
            ovend = rt[:, 5, 8:8 + E]
            ovb = rt[:, 5, 16:16 + E]
            rank = rt[:, 5, 24:24 + C]
            own = rt[:, 5, 32:32 + C]
            far = rt[:, 5, 40:40 + C]
            kk = rt[:, 6, 16:16 + C]
            tk = rt[:, 8, 0:E * K_OVER].rearrange("p (e k) -> p e k", k=K_OVER)
            ok = rt[0:1, 4, 0:E * K_OVER].rearrange("p (s e) -> p s e", e=E)
            prod = rt[:, 0, 0:C * E].rearrange("p (c e) -> p c e", e=E)
            dve.tensor_tensor(tk, cnt.rearrange("p (e o) -> p e o", o=1).broadcast_to((P, E, K_OVER)),
                              capk[:, :].rearrange("p (o k) -> p o k", o=1).broadcast_to((P, E, K_OVER)), ALU.is_gt)
            step(dve.tensor_tensor(prod, rank8, ohe, ALU.mult))
            dve.reduce_sum(nov, tk, AX)
            step(dve.reduce_sum(rank, prod, AX))
            dve.tensor_tensor(tp[:, :, :], tri8[:, :, :],
                              nov.rearrange("p (o e) -> p o e", o=1).broadcast_to((P, E, E)), ALU.mult)
            step(dve.scalar_tensor_tensor(own, ef5, float(CAP), rank, ALU.mult, ALU.add))
            dve.tensor_scalar(far, rank, float(CAP), None, ALU.is_ge)
            step(dve.reduce_sum(ovb, tp[:, :, :], AX))
            step(dve.tensor_tensor(tp[:, 0, :], ovb, shift8[:, :], ALU.add))
            step(dve.tensor_tensor(prod, ohe, tp[:, 0:1, :].broadcast_to((P, C, E)), ALU.mult))
            step(dve.reduce_sum(kk, prod, AX))
            step(dve.tensor_tensor(kk, kk, far, ALU.mult))
            step(dve.tensor_tensor(own, own, kk, ALU.add))
            dve.tensor_copy(slot[:, :], own).then_inc(s_slot, 1)
            dve.tensor_scalar(slot1[:, :], own, float(CAP), None, ALU.add)
            step(dve.scalar_tensor_tensor(ovend, ovb, 1.0 / CAP, nov, ALU.mult, ALU.add))
            dve.tensor_copy(over[0:1, 0:1], ovend[0:1, E - 1:E])
            step(dve.tensor_tensor(ok, ovend[0:1, :].rearrange("p (o e) -> p o e", o=1).broadcast_to((1, K_OVER, E)),
                                   iota8[0:1, 0:K_OVER].rearrange("p (s o) -> p s o", o=1).broadcast_to((1, K_OVER, E)),
                                   ALU.is_le))
            step(dve.reduce_sum(rt[0:1, 6, 32:32 + K_OVER], ok, AX))
            step(dve.tensor_scalar(rt[0:1, 6, 32:32 + K_OVER], rt[0:1, 6, 32:32 + K_OVER], float(E - 1), None, ALU.min))
            dve.tensor_copy(over[0:1, 1:1 + K_OVER], rt[0:1, 6, 32:32 + K_OVER]).then_inc(s_route, 1)

            def tile_in(n_h):
                d.wait_ge(s_hgh, n_h)
                lo(hg[1][:, :, :], hgf[:, :, :], hg[0][:, :, :], s_hgl)

            split_lo(3, 0)
            tile_in(1)
            for c in range(C):
                d.wait_ge(s_b2g, 16 * C)
                d.wait_ge(s_base, C)
                dve.scalar_tensor_tensor(base[:, c, :], x2[:, c, :], wtok[:, c:c + 1], base[:, c, :],
                                         ALU.mult, ALU.add).then_inc(s_base2, 1)


            def tile(e, t, first):
                for k in range(SCH):
                    if k == 0:
                        for n in range(2 if first else 0, 2):
                            split_lo(n, t)
                        if not first:
                            d.wait_ge(s_used, SCH * t)
                            d.wait_ge(s_yst, 16 * t)
                        dve.tensor_copy(ysb[0:CAP, HB:D], ps[0:CAP, 5, 0:HB]).then_inc(s_yev, 1)
                    if 2 <= k <= FCH + 1:
                        d.wait_ge(s_hidT, FCH * t + k - 1)
                        bcol = b1T[:, bass.ds(e * (DF // 128) + JW * (k - 2), JW)]
                        dve.tensor_tensor(bia[:, k % 2, :, :], blocks(2 + k % 2, 128, JW, CAP),
                                          bcol.rearrange("p (j o) -> p j o", o=1).broadcast_to((128, JW, CAP)),
                                          ALU.add).then_inc(s_bia, 1)
                    if k + 2 < SCH and not (first and k < 2):
                        split_lo(k + 2, t)
                    if 2 <= k <= FCH + 1:
                        d.wait_ge(s_hTh2, FCH * t + k - 1)
                        lo(hTT[1][:, JW * (k - 2):JW * (k - 1), :], bia[:, k % 2, :, :],
                           hTT[0][:, JW * (k - 2):JW * (k - 1), :], s_hTl2, relu=True)
                    if k == FCH + 2:
                        tile_in(t + 2)

            tile(0, 0, True)
            with d.Fori(1, E) as t:
                tile(t, t, False)
            d.wait_ge(s_route, 1)
            n_over = d.value_load(over[0:1, 0:1], min_val=0, max_val=K_OVER)
            with d.Fori(0, K_OVER) as s:
                e = d.value_load(over[0:1, bass.ds(s + 1, 1)], min_val=0, max_val=E - 1)
                with d.If(s < n_over):
                    tile(e, s + E, False)
            d.wait_ge(s_used, SCH * (n_over + E))
            d.wait_ge(s_yst, 16 * (n_over + E))
            dve.tensor_copy(ysb[0:CAP, HB:D], ps[0:CAP, 5, 0:HB]).then_inc(s_yev, 1)
            for c in range(C):
                d.wait_ge(s_yg[c], 16)
                dve.scalar_tensor_tensor(x2[:, c, :], x2[:, c, :], wtok[:, c:c + 1], base[:, c, :],
                                         ALU.mult, ALU.add).then_inc(s_fin, 1)

        @block.tensor
        def _(pe):
            mm = nc.tensor.matmul

            def wpart(n, c):
                return [wview(t)[:, c % 3, :] for t in front_w[F_SLOT[n + c // 3]]]

            def count(i, first, last):
                for j in range(EU):
                    pe.wait_ge(s_oh, EU * i + j + 1)
                    for m in range(C):
                        ins = mm(ps[0:P, m, 0:HALF], ohs[:, j, m * P:(m + 1) * P], ohd[:, j, :],
                                 start=first and j == 0, stop=last and j == EU - 1)
                    ins.then_inc(s_ohused, 1)

            at = 0
            for g, steps in enumerate(GROUPS):
                if g:
                    pe.wait_ge(s_cint, g)
                count(at, True, False)
                with pe.Fori(at + 1, at + steps - 1) as i:
                    count(i, False, False)
                count(at + steps - 1, False, True)
                at += steps
                if g == 0:
                    pe.wait_ge(s_const, 9)
                    pe.wait_ge(s_rows, 64)
                    pe.wait_ge(s_b1r, 32)
                    nc.tensor.transpose(ps[:, 6, 0:4 * DC], rows[:, :], ident[0:4 * DC, 0:4 * DC])
                    for i in range(2):
                        ins = nc.tensor.transpose(ps[:, 6, 128 + 96 * i:224 + 96 * i], b1r[:, i, :], ident[0:96, 0:96])
                    ins.then_inc(s_misc, 1)

            def keep_busy(n, left, right, bank=7):
                for _ in range(n):
                    mm(ps[0:left.shape[-1], bank, 0:right.shape[-1]], left, right, start=True, stop=True)

            keep_busy(DECODE_BUSY, onesb[:, :], ohs[:, 0, 0:512])
            pe.wait_ge(s_ones, 1)
            pe.wait_ge(s_Shi, C)
            pe.wait_ge(s_Slo, C)
            for c2 in range(C):
                for c in range(C):
                    for i, t in enumerate(Sd):
                        ins = mm(ps[0:P, 5, 2 * c2:2 * c2 + 2], t[:, c, c2 * P:(c2 + 1) * P], onesr[:, :],
                                 start=c == 0 and i == 0, stop=c == C - 1 and i == 1)
            ins.then_inc(s_deg, 1)
            keep_busy(DEG_BUSY, onesb[:, :], ohs[:, 0, 0:512])
            pe.wait_ge(s_big, 1)
            mm(ps[0:1, 4, 0:2], big[:, 0:1], onesb[:, 0:2], start=True, stop=True).then_inc(s_bigs, 1)
            keep_busy(DEG_BUSY, onesb[:, :], ohs[:, 0, 0:512])
            pe.wait_ge(s_bigi, 1)
            any_big = pe.value_load(bigi[0:1, 0:1], min_val=0, max_val=P)

            def aggregate(r, exact):
                for m in range(DC):
                    if r or m >= 2:
                        pe.wait_ge(s_aggl, r * DC + m - 1)
                    for c in range(C):
                        if not m:
                            if c:
                                keep_busy(ROW_BUSY, Sd[0][:, 0, 0:128], Sd[0][:, 0, 0:512], 3)
                            pe.wait_ge(s_hl if r else s_xnl, c + 1)
                        for half in range(2):
                            xp = [t[:, c, m * 128:(m + 1) * 128] for t in xn]
                            sp_ = [t[:, c, half * HALF:(half + 1) * HALF] for t in Sd]
                            products = pairs(sp_, xp)[0:2 if exact else 3]
                            for i, (rr, l) in enumerate(products):
                                ins = mm(ps[:, 2 * (m % 2) + half, 0:HALF], l, rr, start=c == 0 and i == 0,
                                         stop=c == C - 1 and i == len(products) - 1)
                    ins.then_inc(s_agg, 1)

            def aggregation(r):
                with pe.If(any_big > 0):
                    aggregate(r, False)
                with pe.If(any_big < 1):
                    aggregate(r, True)

            def rows_product(lhs, n, c, bank, ready=None):
                for m in range(DC):
                    if ready and m in ready:
                        pe.wait_ge(*ready[m])
                    for half in range(2):
                        lp = [t[:, m, c * P:(c + 1) * P] for t in lhs]
                        wp = [t[:, half * HB:(half + 1) * HB] for t in wpart(n, m)]
                        for i, (l, rr) in enumerate(pairs(lp, wp)):
                            ins = mm(ps[0:P, bank + half, 0:HB], l, rr,
                                     start=m == 0 and i == 0, stop=m == DC - 1 and i == 2)
                return ins

            pe.wait_ge(s_miscev, 2)
            aggregation(0)
            pe.wait_ge(s_aggl, DC - 1)
            pe.wait_ge(*split(2))
            for c in range(C):
                if c >= 2:
                    pe.wait_ge(s_t, c - 1)
                ins = rows_product(ag, 2 * GNN1, c, 4 + 2 * (c % 2), None if c else {DC - 1: (s_aggl, DC)})
                ins.then_inc(s_xw, 1)
            keep_busy(HIDDEN_BUSY, Sd[0][:, 0, 0:128], Sd[0][:, 0, 0:512], 3)
            aggregation(1)
            pe.wait_ge(s_aggl, 2 * DC - 1)
            pe.wait_ge(*split(4))
            def turn_n1(c):
                pe.wait_ge(s_n1, c + 1)
                if c >= 2:
                    pe.wait_ge(s_aff, DC * (c - 1))
                for m in range(DC):
                    ins = nc.tensor.transpose(blocks(2 * (c % 2), 128, DC, P)[:, m, :], n1[:, c, m * 128:(m + 1) * 128],
                                              ident[0:P, 0:P])
                ins.then_inc(s_n1T, 1)

            for c in range(C):
                pe.wait_ge(s_x1, c - 1) if c >= 2 else pe.wait_ge(s_t, C)
                rows_product(ag, 2 * GNN2, c, 4 + 2 * (c % 2), None if c else {DC - 1: (s_aggl, 2 * DC)}).then_inc(s_xw, 1)
                if c >= 2:
                    turn_n1(c - 2)
            pe.wait_ge(s_x1, C)
            pe.wait_ge(*split(2 * WV + 1))
            for c in range(C):
                pe.wait_ge(s_hTl, c + 1)
                if c >= 2:
                    pe.wait_ge(s_pjl, c - 1)
                rows_product(hT, 2 * WV, c, 4 + 2 * (c % 2), None if c else {DC // 2: split(2 * WV + 2)}
                             ).then_inc(s_pj, 1)
                if c < 2:
                    turn_n1(c + 3)
            pe.wait_ge(s_pad, 2)
            for r, w in enumerate((WQ, WK)):
                pe.wait_ge(*split(2 * w + 2))
                for m in range(PAIRS):
                    if r or m >= 2:
                        pe.wait_ge(s_pjl, C + r * PAIRS + m - 1)
                    for half in range(2):
                        for c in range(DC):
                            wp = [t[:, m * 128:(m + 1) * 128] for t in wpart(2 * w, c)]
                            hp = [t[:, c, half * HALF:(half + 1) * HALF] for t in hT]
                            for i, (l, rr) in enumerate(pairs(wp, hp)):
                                ins = mm(ps[:, 2 * (m % 2) + half, 0:HALF], l, rr,
                                         start=c == 0 and i == 0, stop=c == DC - 1 and i == 2)
                    ins.then_inc(s_pj, 1)
            pe.wait_ge(s_pjl, 2 * PAIRS + C - 1)

            def scores(u):
                h, c = divmod(u, C)
                r0, m = 64 * (h % 2), h // 2
                n = (c + 1) * P + (c + 1) % 2
                if u >= 3:
                    pe.wait_ge(s_ex, u - 2)
                elif u == 2:
                    pe.wait_ge(s_pjl, 2 * PAIRS + C)
                b = score_banks(u)
                for a0, a1 in ((0, min(n, 512)), (512, n)):
                    if a1 <= a0:
                        continue
                    bank = b + a0 // 512
                    qp = [t[r0:r0 + 64, m, c * P:(c + 1) * P] for t in q]
                    kp = [t[r0:r0 + 64, m, a0:a1] for t in k_]
                    d0, d1 = max(c * P, a0), min(n, a1)
                    for i, (l, rr) in enumerate(pairs(qp, kp)):
                        ins = mm(ps[0:P, bank, 0:a1 - a0], l, rr, start=i == 0, stop=i == 2)
                        if i == 0 and d1 > d0:
                            mm(ps[0:P, bank, d0 - a0:d1 - a0], identb[0:P, 0:P], cmask[:, d0 - c * P:d1 - c * P],
                               start=False, stop=False)
                ins.then_inc(s_sc, 1)

            def turn(u):
                pe.wait_ge(s_nm, u + 1)
                if u >= 2:
                    pe.wait_ge(s_trl, u - 1)
                for place, b0, nb in turned_parts(u):
                    for b in range(nb):
                        ins = nc.tensor.transpose(place[:, b, :],
                                                  pr[:, u % 3, (b0 + b) * P:(b0 + b + 1) * P], ident[0:P, 0:P])
                ins.then_inc(s_tr, 1)

            def values(h, half):
                m = h // 2
                pe.wait_ge(s_trl, C * h + (C if half else 3))
                if h:
                    pe.wait_ge(s_pvl, h)
                parts = []
                for b in range(C):
                    t0 = max(b * P - b % 2, half * HALF)
                    t1 = (half + 1) * HALF
                    if t0 < t1:
                        vp = [t[:, b, m * 128:(m + 1) * 128] for t in v]
                        pp = [t[:, b, t0:t1] for t in pT]
                        parts += [(t0, l, rr) for l, rr in pairs(vp, pp)]
                parts = parts[0:2] + parts[3:] + parts[2:3]
                for i, (t0, l, rr) in enumerate(parts):
                    ins = mm(ps[:, 6 + half, t0 - half * HALF:HALF], l, rr, start=i == 0, stop=i == len(parts) - 1)
                ins.then_inc(s_pv, 1)

            scores(0)
            for i in range(UNITS + 4):
                if i + 1 < UNITS:
                    scores(i + 1)
                    if i < 4:
                        keep_busy(FILL_BUSY, k_[0][:, 0, 0:128], k_[0][:, 0, 0:512])
                if i >= 6 and (i - 6) % C == 0:
                    values((i - 6) // C, 0)
                if i >= UNITS:
                    keep_busy(DRAIN_BUSY, v[0][:, 0, 0:128], v[0][:, 0, 0:512], 0)
                if 2 <= i < UNITS + 2:
                    turn(i - 2)
                if i >= 8 and (i - 8) % C == 0:
                    values((i - 8) // C, 1)

            pe.wait_ge(s_pvl, H - 2)
            pe.wait_ge(s_trl, UNITS)
            pe.wait_ge(*split(FRONT))
            def turn_n2(c):
                pe.wait_ge(s_n2, c + 1)
                if c:
                    pe.wait_ge(s_h2T, DC * c)
                for m in range(DC):
                    ins = nc.tensor.transpose(blocks(0, 128, DC, P)[:, m, :], n2[:, c, m * 128:(m + 1) * 128],
                                              ident[0:P, 0:P])
                ins.then_inc(s_n2T, 1)

            def gate_products(c):
                pe.wait_ge(s_h2T, DC * (c + 1))
                for m in range(DC):
                    ins = mm(ps[0:P, 2, c * E:(c + 1) * E], h2T[:, m, c * P:(c + 1) * P], wg[:, m, :],
                             start=m == 0, stop=m == DC - 1)
                return ins

            pe.wait_ge(s_wg, 16)
            for c in range(C):
                if c >= 2:
                    pe.wait_ge(s_x2, c - 1)
                rows_product(q, 2 * WP, c, 4 + 2 * (c % 2), None if c else {DC - 1: (s_pvl, H)}).then_inc(s_wp, 1)
                if c >= 2:
                    gate_products(c - 2)
                if c >= 1:
                    turn_n2(c - 1)
            keep_busy(TURN_BUSY, onesb[:, :], onesb[:, :], 3)
            turn_n2(C - 1)
            gate_products(C - 2)
            gate_products(C - 1).then_inc(s_gate, 1)
            keep_busy(TURN_BUSY, onesb[:, :], onesb[:, :], 3)
            pe.wait_ge(s_oh8, 1)
            ohb = rt[:, 4, 0:C * E // 2].bitcast(BF16).rearrange("p (c e) -> p c e", e=E)
            for c in range(C):
                for b in range(c + 1):
                    mm(ps[0:P, 3, c * E:(c + 1) * E], before[:, :] if b == c else onesb[:, :], ohb[:, b, :],
                       start=b == 0, stop=b == c)
            for b in range(C):
                ins = mm(ps[0:P, 3, C * E:(C + 1) * E], onesb[:, :], ohb[:, b, :], start=b == 0, stop=b == C - 1)
            ins.then_inc(s_rank, 1)

            def tile_in(came, n_in, n_read):
                pe.wait_ge(came, n_in)
                if n_read is not None:
                    pe.wait_ge(s_hgl, n_read)
                for m in range(DC):
                    ins = nc.tensor.transpose(blocks(6, 128, DC, CAP)[:, m, :], hs[0:CAP, m * 128:(m + 1) * 128],
                                              ident[0:CAP, 0:CAP])
                ins.then_inc(s_hgT, 1)

            pe.wait_ge(s_route, 1)
            pe.wait_ge(s_scat, 16 * C)
            keep_busy(LOAD_BUSY, onesb[:, :], onesb[:, :], 3)
            tile_in(s_hs0, 16, None)
            keep_busy(LOAD_BUSY, onesb[:, :], onesb[:, :], 3)

            def tile(t):
                first = isinstance(t, int)
                pe.wait_ge(s_hgl, t + 1)

                def turn_hid(k):
                    pe.wait_ge(s_hidev, FCH * t + k + 1)
                    if not first or k >= 2:
                        pe.wait_ge(s_bia, FCH * t + k - 1)
                    for j in range(JW):
                        ins = nc.tensor.transpose(blocks(2 + k % 2, 128, JW, CAP)[:, j, :],
                                                  hid[0:CAP, k % 2, j * 128:(j + 1) * 128], ident[0:CAP, 0:CAP])
                    ins.then_inc(s_hidT, 1)

                for k in range(FCH):
                    pe.wait_ge(s_mlo, SCH * t + k + 1)
                    if not first or k >= 2:
                        pe.wait_ge(s_hidev, FCH * t + k - 1)
                    i = k % SLOTS
                    for m in range(DC):
                        wp = [w[i][:, m * FW:(m + 1) * FW] for w in (whi, wlo)]
                        lp = [g_[:, m, :] for g_ in hg]
                        for j, (l, rr) in enumerate(pairs(lp, wp)):
                            ins = mm(ps[0:CAP, k % 2, 0:FW], l, rr, start=m == 0 and j == 0, stop=m == DC - 1 and j == 2)
                    ins.then_inc(s_used, 1)
                    if k:
                        turn_hid(k - 1)
                pe.wait_ge(s_yev, 2 * t + 2)
                for k in range(FCH):
                    pe.wait_ge(s_mlo, SCH * t + FCH + k + 1)
                    pe.wait_ge(s_hTl2, FCH * t + k + 1)
                    i = (FCH + k) % SLOTS
                    for half in range(2):
                        for j in range(JW):
                            wp = [w_[:, j, half * HB:(half + 1) * HB] for w_ in (wview(whi[i]), wview(wlo[i]))]
                            lp = [h_[:, JW * k + j, :] for h_ in hTT]
                            for jj, (l, rr) in enumerate(pairs(lp, wp)):
                                ins = mm(ps[0:CAP, 4 + half, 0:HB], l, rr, start=k == 0 and j == 0 and jj == 0,
                                         stop=k == FCH - 1 and j == JW - 1 and jj == 2)
                    ins.then_inc(s_used, 1)
                    if k == 0:
                        turn_hid(FCH - 1)
                    if k == 1:
                        tile_in(s_hs, 16 * t + 16, t + 1)

            tile(0)
            with pe.Fori(1, E) as t:
                tile(t)
            n_over = pe.value_load(over[0:1, 0:1], min_val=0, max_val=K_OVER)
            with pe.Fori(0, K_OVER) as s:
                with pe.If(s < n_over):
                    tile(s + E)


_INS = ["x", "src", "dst", "L0_gnn_W1", "L0_gnn_b1", "L0_gnn_W2", "L0_gnn_b2", "L0_ffn_ln1_g", "L0_ffn_ln1_b",
        "L0_ffn_ln2_g", "L0_ffn_ln2_b", "L0_ffn_Wq", "L0_ffn_Wk", "L0_ffn_Wv", "L0_ffn_Wp", "L0_ffn_bp",
        "L0_ffn_Wg", "L0_ffn_W1", "L0_ffn_b1", "L0_ffn_W2", "L0_ffn_b2"]


def kernel(**inputs):
    import numpy as _np
    import concourse.bacc as _bacc
    from concourse import mybir as _mybir
    from concourse.bass_utils import run_bass_kernel_spmd as _run

    nc = _bacc.Bacc("TRN2", target_bir_lowering=False, num_devices=1)
    arrays, args = {}, []
    for name in _INS:
        a = _np.ascontiguousarray(inputs[name])
        arrays[f"in_{name}"] = a
        args.append(nc.dram_tensor(f"in_{name}", a.shape, _mybir.dt.from_np(a.dtype), kind="ExternalInput").ap())
    out = nc.dram_tensor("out_x", (N, D), F32, kind="ExternalOutput").ap()
    build(nc, *args, out)
    r = _run(nc, [arrays], core_ids=[0])
    return r.results[0]["out_x"]
```
